# Optimizing a Trainium2 kernel written in Bass

```python
import numpy as np
import jax
import jax.numpy as jnp

def _softmax(x, axis=-1):
    return jax.nn.softmax(x, axis=axis)

def _gelu(x):
    return jax.nn.gelu(x, approximate=True)

def _silu(x):
    return jax.nn.silu(x)

def _sigmoid(x):
    return jax.nn.sigmoid(x)

def _layernorm(x, axis=-1, eps=1e-05):
    m = jnp.mean(x, axis=axis, keepdims=True)
    v = jnp.var(x, axis=axis, keepdims=True)
    return (x - m) / jnp.sqrt(v + eps)

def _scatter_add(tgt, idx, src, axis=0):
    return tgt.at[idx].add(src)

def _segment_sum(src, seg, n):
    return jax.ops.segment_sum(src, seg, n)
kernel_name = 'mk_audio_tower_d1_tok_audfeat1024_r4_7e0f7e'

def setup_inputs(seed: int=0):
    np.random.seed(seed)
    _w = jnp.asarray

    def _rec_inputs():
        import jax
        import jax.numpy as jnp
        _rk = jax.random.key(seed)
        x = -7.10856e-05 + 0.999911 * jax.random.normal(jax.random.fold_in(_rk, 1), (64, 256, 256), jnp.float32)
        return x
    x = _rec_inputs()

    def _L0_tok_setup():
        import math
        import jax, jax.numpy as jnp
        import numpy as np
        K = 4
        POS_DIM = 32

        def _fourier_features(pos, dim):
            half = dim // 2
            freqs = jnp.exp(jnp.linspace(0.0, math.log(1000.0), half)).astype(pos.dtype)
            ang = pos[:, None] * freqs
            return jnp.concatenate([jnp.sin(ang), jnp.cos(ang)], axis=-1)
        key = jax.random.key(seed)
        k1, k2, k3 = jax.random.split(key, 3)
        B, M, D = (8, 2048, 256)
        beat_emb = jax.random.normal(k1, (B, M, D), dtype=jnp.float32)
        W = jax.random.normal(k2, (D, D + POS_DIM), dtype=jnp.float32) * 0.02
        b = jax.random.normal(k3, (D,), dtype=jnp.float32) * 0.02
        return {'beat_emb': beat_emb, 'W': W, 'b': b}
    _L0_tok_all = _L0_tok_setup()
    _L0_tok_in = {k: v for k, v in _L0_tok_all.items() if k in ('W', 'b')}
    del _L0_tok_all

    def _L0_attn_setup():
        import math
        import jax, jax.numpy as jnp
        import numpy as np
        B, T, D, H = (4, 512, 256, 16)
        HD = D // H

        def apply_rope(x, base=10000.0):
            _, t, _, dh = x.shape
            half = dh // 2
            inv_freq = 1.0 / base ** (jnp.arange(half, dtype=jnp.float32) / float(half))
            pos = jnp.arange(t, dtype=jnp.float32)
            angles = pos[:, None] * inv_freq[None, :]
            sin = jnp.sin(angles)[None, :, None, :]
            cos = jnp.cos(angles)[None, :, None, :]
            x1 = x[..., :half]
            x2 = x[..., half:2 * half]
            rot1 = x1 * cos - x2 * sin
            rot2 = x1 * sin + x2 * cos
            return jnp.concatenate([rot1, rot2, x[..., 2 * half:]], axis=-1)
        key = jax.random.key(seed)
        k1, k2, k3 = jax.random.split(key, 3)
        x = jax.random.normal(k1, (B, T, D), dtype=jnp.float32)
        Wqkv = jax.random.normal(k2, (D, 3 * D), dtype=jnp.float32) / math.sqrt(D)
        Wo = jax.random.normal(k3, (D, D), dtype=jnp.float32) / math.sqrt(D)
        bo = jnp.zeros((D,), dtype=jnp.float32)
        return {'x': x, 'Wqkv': Wqkv, 'Wo': Wo, 'bo': bo}
    _L0_attn_all = _L0_attn_setup()
    _L0_attn_in = {k: v for k, v in _L0_attn_all.items() if k in ('Wqkv', 'Wo', 'bo')}
    del _L0_attn_all

    def _L0_ffn_setup():
        import jax, jax.numpy as jnp
        import numpy as np
        B, N, D = (4, 512, 256)
        SPARSITY = 0.01
        key = jax.random.key(seed)
        k1, k2, k3 = jax.random.split(key, 3)
        x = jax.random.normal(k1, (B, N, D), dtype=jnp.float32)
        spatial = jax.random.normal(k2, (D, D), dtype=jnp.float32) * 0.02
        freq = jnp.fft.fft(spatial, axis=-1)
        k = int(D * SPARSITY)
        mag = jnp.abs(freq)
        kth = jax.lax.top_k(mag, k)[0][:, -1:]
        w_sparse = jnp.where(mag >= kth, freq, 0.0 + 0j)
        bias = jax.random.normal(k3, (D,), dtype=jnp.float32) * 0.01
        return {'x': x, 'w_freq_real': jnp.real(w_sparse).astype(jnp.float32), 'w_freq_imag': jnp.imag(w_sparse).astype(jnp.float32), 'bias': bias}
    _L0_ffn_all = _L0_ffn_setup()
    _L0_ffn_in = {k: v for k, v in _L0_ffn_all.items() if k in ('w_freq_real', 'w_freq_imag', 'bias')}
    del _L0_ffn_all
    return {'x': x, 'L0_tok_W': _L0_tok_in['W'], 'L0_tok_b': _L0_tok_in['b'], 'L0_attn_Wqkv': _L0_attn_in['Wqkv'], 'L0_attn_Wo': _L0_attn_in['Wo'], 'L0_attn_bo': _L0_attn_in['bo'], 'L0_ffn_w_freq_real': _L0_ffn_in['w_freq_real'], 'L0_ffn_w_freq_imag': _L0_ffn_in['w_freq_imag'], 'L0_ffn_bias': _L0_ffn_in['bias']}

def reference(x, L0_tok_W, L0_tok_b, L0_attn_Wqkv, L0_attn_Wo, L0_attn_bo, L0_ffn_w_freq_real, L0_ffn_w_freq_imag, L0_ffn_bias):
    import jax
    import jax.numpy as jnp

    def _L0_tok_ref(beat_emb, W, b):
        import math
        import jax, jax.numpy as jnp
        import numpy as np
        K = 4
        POS_DIM = 32

        def _fourier_features(pos, dim):
            half = dim // 2
            freqs = jnp.exp(jnp.linspace(0.0, math.log(1000.0), half)).astype(pos.dtype)
            ang = pos[:, None] * freqs
            return jnp.concatenate([jnp.sin(ang), jnp.cos(ang)], axis=-1)
        B, M, D = beat_emb.shape
        Mb = (M + K - 1) // K
        pad = Mb * K - M
        x = jnp.pad(beat_emb, ((0, 0), (0, pad), (0, 0))) if pad else beat_emb
        sums = x.reshape(B, Mb, K, D).sum(axis=2)
        counts = jnp.minimum(K, M - jnp.arange(Mb) * K).astype(beat_emb.dtype)
        out = sums / counts[None, :, None]
        idx = jnp.arange(Mb, dtype=beat_emb.dtype)
        pos = jnp.clip(idx / max(1, Mb - 1), 0.0, 1.0)
        ff = _fourier_features(pos, POS_DIM)
        ff = jnp.broadcast_to(ff[None], (B, Mb, POS_DIM))
        h = jnp.concatenate([out, ff], axis=-1)
        return jnp.einsum('bmi,oi->bmo', h, W) + b

    def _L0_attn_ref(x, Wqkv, Wo, bo):
        import math
        import jax, jax.numpy as jnp
        import numpy as np
        B, T, D, H = (4, 512, 256, 16)
        HD = D // H

        def apply_rope(x, base=10000.0):
            _, t, _, dh = x.shape
            half = dh // 2
            inv_freq = 1.0 / base ** (jnp.arange(half, dtype=jnp.float32) / float(half))
            pos = jnp.arange(t, dtype=jnp.float32)
            angles = pos[:, None] * inv_freq[None, :]
            sin = jnp.sin(angles)[None, :, None, :]
            cos = jnp.cos(angles)[None, :, None, :]
            x1 = x[..., :half]
            x2 = x[..., half:2 * half]
            rot1 = x1 * cos - x2 * sin
            rot2 = x1 * sin + x2 * cos
            return jnp.concatenate([rot1, rot2, x[..., 2 * half:]], axis=-1)
        b, t, d = x.shape
        qkv = x @ Wqkv
        q, k, v = jnp.split(qkv, 3, axis=-1)
        q = q.reshape(b, t, H, HD)
        k = k.reshape(b, t, H, HD)
        v = v.reshape(b, t, H, HD)
        q = apply_rope(q)
        k = apply_rope(k)
        q = q / jnp.sqrt(jnp.sum(q * q, axis=-1, keepdims=True) + 1e-06)
        k = k / jnp.sqrt(jnp.sum(k * k, axis=-1, keepdims=True) + 1e-06)
        attn = jnp.einsum('bthd,bshd->bhts', q, k) / math.sqrt(HD)
        attn = jax.nn.softmax(attn, axis=-1)
        out = jnp.einsum('bhts,bshd->bthd', attn, v).reshape(b, t, d)
        return out @ Wo + bo

    def _L0_ffn_ref(x, w_freq_real, w_freq_imag, bias):
        import jax, jax.numpy as jnp
        import numpy as np
        B, N, D = (4, 512, 256)
        SPARSITY = 0.01
        w = jax.lax.complex(w_freq_real, w_freq_imag)
        x_freq = jnp.fft.fft(x, axis=-1)
        y_freq = jnp.einsum('bnd,do->bno', x_freq, w)
        y = jnp.real(jnp.fft.ifft(y_freq, axis=-1))
        return y + bias
    h = _L0_tok_ref(x, L0_tok_W, L0_tok_b)
    h = h + _L0_attn_ref(_layernorm(h, axis=-1), L0_attn_Wqkv, L0_attn_Wo, L0_attn_bo)
    h = h + _L0_ffn_ref(_layernorm(h, axis=-1), L0_ffn_w_freq_real, L0_ffn_w_freq_imag, L0_ffn_bias)
    return h

_drawn_inputs = setup_inputs


def setup_inputs(seed=0):
    import zlib

    import numpy as np

    out = dict(_drawn_inputs(seed))
    spreads = {'L0_attn_bo': (0.0, 0.1)}
    factors = {'L0_ffn_bias': 4.383}
    for name, (base, spread) in spreads.items():
        noise = np.random.default_rng([zlib.crc32(name.encode()), seed]).standard_normal(out[name].shape)
        drawn = base * np.exp(spread * noise) if base else spread * noise
        out[name] = jnp.asarray(drawn.astype(out[name].dtype))
    for name, factor in factors.items():
        out[name] = (out[name] * factor).astype(out[name].dtype)
    return out
```

```python
from contextlib import ExitStack

import numpy as np

import concourse.bass as bass
from concourse import mybir

F32 = mybir.dt.float32
F32R = mybir.dt.float32r
ALU = mybir.AluOpType
ACT = mybir.ActivationFunctionType
AX_X = mybir.AxisListType.X

P = 128
K = 4
D = 256
C = D // P
T = 64
S = P // T
HD = 16
H = D // HD
R = P // 32
POS = 32
LN_EPS = 1e-5
QK_EPS = 1e-6
RING = 3


def audio_tower(nc, x, w_tok, b_tok, w_qkv, w_o, b_o, w_re, w_im, b_ffn, dft, consts, pos_feat, out):
    tiles = x.shape[0] * x.shape[1] * x.shape[2] // (K * D * P)
    x_tiles = x.rearrange("b (t k) d -> (b t) (k d)", k=K).rearrange("(n p) f -> n p f", p=P)
    out_tiles = out.rearrange("b t d -> (b t) d").rearrange("(n p) d -> n p d", p=P)

    with ExitStack() as ctx:
        def sb(name, shape, dt=F32):
            return ctx.enter_context(nc.sbuf_tensor(name, shape, dt))

        def sem(name):
            return ctx.enter_context(nc.semaphore(name))

        bank01 = ctx.enter_context(nc.psum_tensor("bank01", [P, 2, 512], F32))
        bank2 = ctx.enter_context(nc.psum_tensor("bank2", [P, 512], F32))
        bank3 = ctx.enter_context(nc.psum_tensor("bank3", [P, 512], F32))
        ps_scores = ctx.enter_context(nc.psum_tensor("ps_scores", [P, R, 512], F32))
        ps_av = bank01[:, :, 0:P].rearrange("p s (c t) -> p s c t", c=C)
        ps_den = ps_scores[:, 1:1 + S, 0:P].rearrange("p s (c t) -> p s c t", c=C)
        ps_attn = bank01[:, 0, 0:D]
        ps_h1T = bank01[:, 0, 0:D].rearrange("p (c t) -> p c t", c=C)
        ps_pT = bank01[:, 1, 0:D].rearrange("p (c t) -> p c t", c=C)
        ps_h = bank2[:, 0:D]
        ps_hT = bank2[:, 0:D].rearrange("p (c t) -> p c t", c=C)
        ps_v = bank2[:, 0:D]
        ps_qk = bank3[:, :]
        ps_qkT = bank3[:, :].rearrange("p (c t) -> p c t", c=2 * C)
        ps_mix = ps_scores[:, 0, 0:D]

        ident = sb("ident", [P, P])
        const = sb("const", [P, 2 * HD + 2 + 64])
        rope_cos, rope_sin = const[:, 0:HD], const[:, HD:2 * HD]
        head_mask = const[:, 2 * HD:2 * HD + 2]
        den_sel = const[:, 2 * HD + 2:].rearrange("p (a m) -> p a m", a=2)
        bo_rows = sb("bo_rows", [P, D])
        bf_rows = sb("bf_rows", [P, D])
        w_raw = sb("w_raw", [P, C, D + 3 * D + D])
        w_pos = sb("w_pos", [POS + 1, D])
        feat = sb("feat", [POS + 1, P])
        pos_rows = sb("pos_rows", [P, D])
        dft_sb = sb("dft_sb", [P, C, 3 * D])
        w_freq = sb("w_freq", [P, 2, C, D])
        half_mix = sb("half_mix", [P, C, 2 * D])
        W_ALL = D + 3 * D + D + D
        TOK, QK, V, O, MIX = 0, D, 3 * D, 4 * D, 5 * D
        w_hi = sb("w_hi", [P, C, W_ALL], F32R)
        w_lo = sb("w_lo", [P, C, W_ALL], F32R)

        x_in = sb("x_in", [P, RING, K * D])
        pair_sum = sb("pair_sum", [P, 2 * D])
        pooled = sb("pooled", [P, D])
        pT_hi, pT_lo = sb("pT_hi", [P, C, P], F32R), sb("pT_lo", [P, C, P], F32R)
        h = sb("h", [P, D])
        h_bo = sb("h_bo", [P, RING, D])
        h_bn, h_mv, h_var = sb("h_bn", [P, 6]), sb("h_mv", [P, 2]), sb("h_var", [P, 1])
        h_ln, h_rs0, h_nt, h_rs = (sb(n, [P, 1]) for n in ("h_ln", "h_rs0", "h_nt", "h_rs"))
        xn = sb("xn", [P, D])
        hT_hi, hT_lo = sb("hT_hi", [P, C, P], F32R), sb("hT_lo", [P, C, P], F32R)
        v_pad = sb("v_pad", [P, RING, H // 2, 4, HD])
        sq = sb("sq", [P, 2 * D])
        q_cos, q_sin, q_rot, qk_n = (sb(n, [P, 2 * D]) for n in ("q_cos", "q_sin", "q_rot", "qk_n"))
        ss, ss_ln, ss_rs0, ss_nt, ss_nu, ss_rs = (sb(n, [P, 2 * H]) for n in
                                                  ("ss", "ss_ln", "ss_rs0", "ss_nt", "ss_nu", "ss_rs"))
        kT = sb("kT", [P, C, P])
        q_mask = sb("q_mask", [P, C, 2, P])
        e = sb("e", [P, R, C, 2, T])
        den_r = sb("den_r", [P, S, C, T])
        o_f = sb("o_f", [P, C, P])
        o_hi, o_lo = sb("o_hi", [P, C, P], F32R), sb("o_lo", [P, C, P], F32R)
        h1 = sb("h1", [P, D])
        h1_bf = sb("h1_bf", [P, RING, D])
        g_bn, g_mv, g_var = sb("g_bn", [P, 6]), sb("g_mv", [P, 2]), sb("g_var", [P, 1])
        g_ln, g_rs0, g_nt, g_rs = (sb(n, [P, 1]) for n in ("g_ln", "g_rs0", "g_nt", "g_rs"))
        xn1 = sb("xn1", [P, D])
        h1T_hi, h1T_lo = sb("h1T_hi", [P, C, P], F32R), sb("h1T_lo", [P, C, P], F32R)
        y = sb("y", [P, RING, D])
        eps_ln = sb("eps_ln", [P, 1])

        const_in = sem("const_in")
        w_in = sem("w_in")
        freq_in = sem("freq_in")
        zeroed = sem("zeroed")
        ident_ok = sem("ident_ok")
        w_hi_ok, w_lo_ok = sem("w_hi_ok"), sem("w_lo_ok")
        mix_hi_ok, mix_lo_ok = sem("mix_hi_ok"), sem("mix_lo_ok")
        pos_mm, pos_ok = sem("pos_mm"), sem("pos_ok")
        half_mm, half_ok, mix_mm = sem("half_mm"), sem("half_ok"), sem("mix_mm")
        x_ok = [sem(f"x_ok{i}") for i in range(RING)]
        out_sent = [sem(f"out_sent{i}") for i in range(RING)]
        pair_ok, pooled_ok = sem("pair_ok"), sem("pooled_ok")
        pT_mm, pT_hi_ok, pT_lo_ok = sem("pT_mm"), sem("pT_hi_ok"), sem("pT_lo_ok")
        h_mm, h_ok, h_bo_ok = sem("h_mm"), sem("h_ok"), sem("h_bo_ok")
        h_bn_ok, h_mv_ok, h_var_ok, h_ln_ok = sem("h_bn_ok"), sem("h_mv_ok"), sem("h_var_ok"), sem("h_ln_ok")
        h_rs0_ok, h_nt_ok, h_nu_ok, h_rs_ok = sem("h_rs0_ok"), sem("h_nt_ok"), sem("h_nu_ok"), sem("h_rs_ok")
        xn_ok, hT_mm, hT_hi_ok, hT_lo_ok = sem("xn_ok"), sem("hT_mm"), sem("hT_hi_ok"), sem("hT_lo_ok")
        v_mm, v_ok, qk_mm, sq_ok = sem("v_mm"), sem("v_ok"), sem("qk_mm"), sem("sq_ok")
        cos_ok, ss_sum_ok = sem("cos_ok"), sem("ss_sum_ok")
        rope_ok, rot_ok, ss_ok, ss_ln_ok = sem("rope_ok"), sem("rot_ok"), sem("ss_ok"), sem("ss_ln_ok")
        ss_rs0_ok, ss_nt_ok, ss_nu_ok, ss_nw_ok, ss_rs_ok = (
            sem(n) for n in ("ss_rs0_ok", "ss_nt_ok", "ss_nu_ok", "ss_nw_ok", "ss_rs_ok"))
        qk_n_ok, qkT_mm, qkT_ok = sem("qk_n_ok"), sem("qkT_mm"), sem("qkT_ok")
        scores_mm, e_ok = sem("scores_mm"), sem("e_ok")
        den_mm, av_mm, den_r_ok, o_f_ok, o_hi_ok, o_lo_ok = (
            sem(n) for n in ("den_mm", "av_mm", "den_r_ok", "o_f_ok", "o_hi_ok", "o_lo_ok"))
        attn_mm, h1_ok, h1_bf_ok = sem("attn_mm"), sem("h1_ok"), sem("h1_bf_ok")
        g_bn_ok, g_mv_ok, g_var_ok, g_ln_ok = sem("g_bn_ok"), sem("g_mv_ok"), sem("g_var_ok"), sem("g_ln_ok")
        g_rs0_ok, g_nt_ok, g_nu_ok, g_rs_ok = sem("g_rs0_ok"), sem("g_nt_ok"), sem("g_nu_ok"), sem("g_rs_ok")
        xn1_ok, h1T_mm, h1T_hi_ok, h1T_lo_ok = sem("xn1_ok"), sem("h1T_mm"), sem("h1T_hi_ok"), sem("h1T_lo_ok")
        y_mm, y_ok = sem("y_mm"), sem("y_ok")

        block = ctx.enter_context(nc.Block())

        AHEAD = 4
        FIRST = 1
        LAST = FIRST + (tiles - AHEAD - FIRST) // RING * RING

        def steps(eng, step):
            for j in range(-2, FIRST):
                step(j, j)
            with eng.Fori(FIRST, LAST - RING + 1, RING) as j:
                for u in range(RING):
                    step(j + u, FIRST + u)
            for j in range(LAST, tiles + 1):
                step(j, j)

        def phases(s):
            return s + 2 < tiles, -1 <= s < tiles - 1, 0 <= s < tiles, 1 <= s

        def x_count(j, s):
            return 16 * ((j - s % RING) // RING + 1)

        @block.sync
        def _(sp):
            for n in range(AHEAD - 2):
                sp.dma_start(x_in[:, n, :], x_tiles[n]).then_inc(x_ok[n], 16)
                if n == 0:
                    sp.dma_start(w_raw[:, :, 0:D], w_tok[0:D, :].rearrange("(c p) n -> p c n", p=P)).then_inc(w_in, 16)
                    sp.dma_start(w_raw[:, :, D:4 * D], w_qkv.rearrange("(c p) n -> p c n", p=P)).then_inc(w_in, 16)
                    sp.dma_start(w_raw[:, :, 4 * D:5 * D], w_o.rearrange("(c p) n -> p c n", p=P)).then_inc(w_in, 16)

            def step(j, s):
                front, middle, back, mix = phases(s)
                if s + AHEAD < tiles:
                    n = (s + AHEAD) % RING
                    if s + AHEAD >= RING:
                        sp.wait_ge(pooled_ok, j + AHEAD - RING + 1)
                    sp.dma_start(x_in[:, n, :], x_tiles[j + AHEAD]).then_inc(x_ok[n], 16)
                if mix:
                    sp.wait_ge(y_ok, j)
                    sp.dma_start(out_tiles[j - 1], y[:, (s - 1) % RING, :]).then_inc(out_sent[(s - 1) % RING], 16)

            steps(sp, step)
            for n in range(RING):
                sp.wait_ge(out_sent[n], 16 * len(range(n, tiles, RING)))

        @block.gpsimd
        def _(pool):
            nc.gpsimd.memset(ident[:], 0.0).then_inc(zeroed, 1)
            pool.wait_ge(zeroed, 1)
            nc.gpsimd.affine_select(out=ident[:], in_=ident[:], compare_op=ALU.not_equal, fill=1.0, base=0,
                                    pattern=[[-1, P]], channel_multiplier=1).then_inc(ident_ok, 1)
            nc.gpsimd.memset(v_pad[:], 0.0).then_inc(zeroed, 1)
            nc.gpsimd.memset(eps_ln[:], 0.0).then_inc(zeroed, 1)

            def pool_frames(j, s):
                if s >= 1:
                    pool.wait_ge(pT_mm, j)
                pool.wait_ge(x_ok[s % RING], x_count(j, s))
                nc.gpsimd.tensor_tensor(pair_sum[:], x_in[:, s % RING, 0:2 * D], x_in[:, s % RING, 2 * D:4 * D],
                                        ALU.add).then_inc(pair_ok, 1)
                pool.wait_ge(pair_ok, j + 1)
                nc.gpsimd.tensor_tensor(pooled[:], pair_sum[:, 0:D], pair_sum[:, D:2 * D],
                                        ALU.add).then_inc(pooled_ok, 1)

            def step(j, s):
                front, middle, back, mix = phases(s)
                if middle:
                    if s >= 0:
                        pool.wait_ge(qkT_mm, j + 1)
                    pool.wait_ge(ss_rs_ok, j + 2)
                    pool.wait_ge(rot_ok, j + 2)
                    nc.gpsimd.tensor_tensor(
                        qk_n[:].rearrange("p (h d) -> p h d", d=HD), q_rot[:].rearrange("p (h d) -> p h d", d=HD),
                        ss_rs[:].unsqueeze(2).to_broadcast([P, 2 * H, HD]), ALU.mult).then_inc(qk_n_ok, 1)
                if front:
                    if s >= 1:
                        pool.wait_ge(h1_ok, j)
                    if s == -2:
                        pool.wait_ge(const_in, 16 * 5)
                    pool.wait_ge(h_ok, j + 3)
                    nc.gpsimd.tensor_tensor(h_bo[:, (s + 2) % RING, :], h[:], bo_rows[:], ALU.add).then_inc(h_bo_ok, 1)
                if back:
                    pool.wait_ge(o_hi_ok, j + 1)
                    if s >= 1:
                        pool.wait_ge(attn_mm, j)
                    nc.gpsimd.tensor_tensor(o_lo[:], o_f[:], o_hi[:].bitcast(F32), ALU.subtract).then_inc(o_lo_ok, 1)
                if front and s + 3 < tiles:
                    pool_frames(j + 3, s + 3)
                if back:
                    if s >= RING:
                        pool.wait_ge(y_ok, j - RING + 1)
                    pool.wait_ge(h1_ok, j + 1)
                    nc.gpsimd.tensor_tensor(h1_bf[:, s % RING, :], h1[:], bf_rows[:], ALU.add).then_inc(h1_bf_ok, 1)
                if front:
                    if s >= -1:
                        pool.wait_ge(qk_n_ok, j + 2)
                    pool.wait_ge(rope_ok, j + 3)
                    nc.gpsimd.tensor_tensor(q_rot[:], q_cos[:], q_sin[:], ALU.add).then_inc(rot_ok, 1)

            pool_frames(0, 0)
            steps(pool, step)

        @block.scalar
        def _(act):
            nc.scalar.preload_act_table_set("natural_log_exp_and_others")
            act.dma_start(const[:], consts).then_inc(const_in, 16)
            act.dma_start(feat[:], pos_feat).then_inc(const_in, 16)
            act.dma_start(w_pos[0:POS, :], w_tok[D:D + POS, :]).then_inc(const_in, 16)
            act.dma_start(w_pos[POS:POS + 1, :], b_tok.rearrange("(a n) -> a n", a=1)).then_inc(const_in, 16)
            act.dma_start(bo_rows[:], b_o.rearrange("(a n) -> a n", a=1).to_broadcast([P, D])).then_inc(const_in, 16)
            act.dma_start(bf_rows[:], b_ffn.rearrange("(a n) -> a n", a=1).to_broadcast([P, D])).then_inc(const_in, 16)
            act.dma_start(w_freq[:, 0], w_re.rearrange("(c p) n -> p c n", p=P)).then_inc(freq_in, 16)
            act.dma_start(w_freq[:, 1], w_im.rearrange("(c p) n -> p c n", p=P)).then_inc(freq_in, 16)
            act.dma_start(dft_sb[:], dft.rearrange("(c p) n -> p c n", p=P)).then_inc(freq_in, 16)
            act.wait_ge(w_in, 16 * 3)
            nc.scalar.activation(w_hi[:, :, TOK:QK], w_raw[:, :, 0:D], ACT.Copy, scale=1.0 / K).then_inc(w_hi_ok, 1)
            nc.scalar.activation(w_hi[:, :, QK:MIX], w_raw[:, :, D:5 * D], ACT.Copy).then_inc(w_hi_ok, 1)

            def high(src, dst, done):
                nc.scalar.activation(dst[:], src, ACT.Copy).then_inc(done, 1)

            act.wait_ge(pT_mm, 1)
            high(ps_pT, pT_hi, pT_hi_ok)

            def rsqrt(src, ln, rs0, ready, n, ln_ok, rs0_ok):
                act.wait_ge(ready, n)
                nc.scalar.activation(ln[:], src[:], ACT.Ln).then_inc(ln_ok, 1)
                act.wait_ge(ln_ok, n)
                nc.scalar.activation(rs0[:], ln[:], ACT.Exp, scale=-0.5).then_inc(rs0_ok, 1)

            def step(j, s):
                front, middle, back, mix = phases(s)
                if front:
                    if s >= -1:
                        act.wait_ge(h_rs_ok, j + 2)
                    rsqrt(h_var, h_ln, h_rs0, h_var_ok, j + 3, h_ln_ok, h_rs0_ok)
                if middle:
                    act.wait_ge(qkT_mm, j + 2)
                    if s == -1:
                        act.wait_ge(const_in, 16 * 5)
                    nc.scalar.activation(kT[:], ps_qkT[:, C:2 * C, :], ACT.Copy).then_inc(qkT_ok, 1)
                    for a in range(2):
                        nc.scalar.activation(q_mask[:, :, a, :], ps_qkT[:, 0:C, :], ACT.Copy,
                                             scale=head_mask[:, a:a + 1]).then_inc(qkT_ok, 1)
                if back:
                    act.wait_ge(o_f_ok, j + 1)
                    if s >= 1:
                        act.wait_ge(attn_mm, j)
                    high(o_f[:], o_hi, o_hi_ok)
                if front:
                    act.wait_ge(hT_mm, j + 3)
                    high(ps_hT, hT_hi, hT_hi_ok)
                if middle:
                    act.wait_ge(scores_mm, j + 2)
                    nc.scalar.activation(e[:].rearrange("p r c a t -> p r (c a t)"), ps_scores[:, :, 0:2 * P],
                                         ACT.Exp, scale=HD ** -0.5).then_inc(e_ok, 1)
                if front and s + 3 < tiles:
                    act.wait_ge(pT_mm, j + 4)
                    high(ps_pT, pT_hi, pT_hi_ok)
                if back:
                    if s >= 1:
                        act.wait_ge(g_rs_ok, j)
                    rsqrt(g_var, g_ln, g_rs0, g_var_ok, j + 1, g_ln_ok, g_rs0_ok)
                if front:
                    act.wait_ge(v_mm, j + 3)
                    if s == -2:
                        act.wait_ge(zeroed, 3)
                    nc.scalar.activation(v_pad[:, (s + 2) % RING, :, 0:4:3, :],
                                         ps_v.rearrange("p (h a d) -> p h a d", a=2, d=HD), ACT.Copy).then_inc(v_ok, 1)
                    act.wait_ge(qk_mm, j + 3)
                    if s >= -1:
                        act.wait_ge(ss_sum_ok, j + 2)
                    nc.scalar.activation(sq[:], ps_qk, ACT.Square).then_inc(sq_ok, 1)
                if back:
                    act.wait_ge(h1T_mm, j + 1)
                    high(ps_h1T, h1T_hi, h1T_hi_ok)
                if front:
                    if s >= -1:
                        act.wait_ge(ss_rs_ok, j + 2)
                    rsqrt(ss, ss_ln, ss_rs0, ss_ok, j + 3, ss_ln_ok, ss_rs0_ok)
                if s == -2:
                    act.wait_ge(mix_mm, 1)
                    nc.scalar.activation(w_hi[:, :, MIX:], bank01[:, :, 0:D], ACT.Copy).then_inc(mix_hi_ok, 1)

            steps(act, step)

        @block.vector
        def _(dve):
            def low(src, hi, dst, hi_ok, n, done):
                dve.wait_ge(hi_ok, n)
                nc.vector.tensor_tensor(dst[:], src, hi[:].bitcast(F32), ALU.subtract).then_inc(done, 1)

            def moments(src, bn, mv, var, n, src_ok, bn_ok, mv_ok, var_ok):
                dve.wait_ge(src_ok, n)
                nc.vector.bn_stats(bn[:], src[:]).then_inc(bn_ok, 1)
                dve.wait_ge(pos_ok, 1)
                dve.wait_ge(bn_ok, n)
                nc.vector.bn_aggr(mv[:], bn[:]).then_inc(mv_ok, 1)
                dve.wait_ge(mv_ok, n)
                nc.vector.tensor_scalar(var[:], mv[:, 1:2], LN_EPS, None, ALU.add).then_inc(var_ok, 1)

            def normalise(src, mv, var, rs0, nt, rs, dst, n, rs0_ok, nt_ok, nu_ok, rs_ok, dst_ok):
                dve.wait_ge(rs0_ok, n)
                nc.vector.tensor_scalar(nt[:], rs0[:], rs0[:, 0:1], var[:, 0:1], ALU.mult, ALU.mult).then_inc(nt_ok, 1)
                dve.wait_ge(nt_ok, n)
                nc.vector.tensor_scalar(rs[:], nt[:], -0.5, 1.5, ALU.mult, ALU.add).then_inc(nu_ok, 1)
                dve.wait_ge(nu_ok, n)
                nc.vector.tensor_tensor(rs[:], rs[:], rs0[:], ALU.mult).then_inc(rs_ok, 1)
                dve.wait_ge(rs_ok, n)
                nc.vector.tensor_scalar(dst[:], src[:], mv[:, 0:1], rs[:, 0:1], ALU.subtract, ALU.mult).then_inc(dst_ok, 1)

            def step(j, s):
                front, middle, back, mix = phases(s)
                if front:
                    dve.wait_ge(h_mm, j + 3)
                    if s == -2:
                        dve.wait_ge(pos_ok, 1)
                    if s >= -1:
                        dve.wait_ge(h_bo_ok, j + 2)
                    nc.vector.tensor_tensor(h[:], ps_h, pos_rows[:], ALU.add).then_inc(h_ok, 1)
                    moments(h, h_bn, h_mv, h_var, j + 3, h_ok, h_bn_ok, h_mv_ok, h_var_ok)
                if middle:
                    n = j + 2
                    dve.wait_ge(ss_rs0_ok, n)
                    nc.vector.tensor_tensor(ss_nt[:], ss_rs0[:], ss_rs0[:], ALU.mult).then_inc(ss_nt_ok, 1)
                    dve.wait_ge(ss_nt_ok, n)
                    nc.vector.tensor_tensor(ss_nu[:], ss_nt[:], ss[:], ALU.mult).then_inc(ss_nu_ok, 1)
                    dve.wait_ge(ss_nu_ok, n)
                    nc.vector.tensor_scalar(ss_nt[:], ss_nu[:], -0.5, 1.5, ALU.mult, ALU.add).then_inc(ss_nw_ok, 1)
                    dve.wait_ge(ss_nw_ok, n)
                    if s >= 0:
                        dve.wait_ge(qk_n_ok, j + 1)
                    nc.vector.tensor_tensor(ss_rs[:], ss_nt[:], ss_rs0[:], ALU.mult).then_inc(ss_rs_ok, 1)
                if front:
                    normalise(h, h_mv, h_var, h_rs0, h_nt, h_rs, xn, j + 3,
                              h_rs0_ok, h_nt_ok, h_nu_ok, h_rs_ok, xn_ok)
                if mix:
                    dve.wait_ge(y_mm, j)
                    dve.wait_ge(h1_bf_ok, j)
                    if s - 1 >= RING:
                        dve.wait_ge(out_sent[(s - 1) % RING], x_count(j - 1 - RING, s - 1 - RING))
                    nc.vector.tensor_tensor(y[:, (s - 1) % RING, :], ps_mix, h1_bf[:, (s - 1) % RING, :],
                                            ALU.add).then_inc(y_ok, 1)
                if back:
                    dve.wait_ge(den_mm, j + 1)
                    nc.vector.reciprocal(den_r[:], ps_den).then_inc(den_r_ok, 1)
                    dve.wait_ge(den_r_ok, j + 1)
                    dve.wait_ge(av_mm, j + 1)
                    if s >= 1:
                        dve.wait_ge(o_lo_ok, j)
                    nc.vector.tensor_tensor(o_f[:].rearrange("p c (s t) -> p s c t", s=S), ps_av, den_r[:],
                                            ALU.mult).then_inc(o_f_ok, 1)
                if front:
                    low(ps_hT, hT_hi, hT_lo, hT_hi_ok, j + 3, hT_lo_ok)
                if back:
                    dve.wait_ge(attn_mm, j + 1)
                    dve.wait_ge(h_bo_ok, j + 1)
                    if s >= 1:
                        dve.wait_ge(h1_bf_ok, j)
                    nc.vector.tensor_tensor(h1[:], ps_attn, h_bo[:, s % RING, :], ALU.add).then_inc(h1_ok, 1)
                    moments(h1, g_bn, g_mv, g_var, j + 1, h1_ok, g_bn_ok, g_mv_ok, g_var_ok)
                if front and s + 3 < tiles:
                    low(ps_pT, pT_hi, pT_lo, pT_hi_ok, j + 4, pT_lo_ok)
                if back:
                    normalise(h1, g_mv, g_var, g_rs0, g_nt, g_rs, xn1, j + 1,
                              g_rs0_ok, g_nt_ok, g_nu_ok, g_rs_ok, xn1_ok)
                if front:
                    dve.wait_ge(sq_ok, j + 3)
                    if s >= -1:
                        dve.wait_ge(rot_ok, j + 2)
                    nc.vector.tensor_tensor(
                        q_cos[:].rearrange("p (h d) -> p h d", d=HD), ps_qk.rearrange("p (h d) -> p h d", d=HD),
                        rope_cos.unsqueeze(1).to_broadcast([P, 2 * H, HD]), ALU.mult).then_inc(cos_ok, 1)
                    for a in range(2):
                        half = slice(a * HD // 2, (a + 1) * HD // 2)
                        other = slice((1 - a) * HD // 2, (2 - a) * HD // 2)
                        last = nc.vector.tensor_tensor(
                            q_sin[:].rearrange("p (h d) -> p h d", d=HD)[:, :, half],
                            ps_qk.rearrange("p (h d) -> p h d", d=HD)[:, :, other],
                            rope_sin[:, half].unsqueeze(1).to_broadcast([P, 2 * H, HD // 2]), ALU.mult)
                    last.then_inc(rope_ok, 1)
                    nc.vector.tensor_reduce(ss[:], sq[:].rearrange("p (h d) -> p h d", d=HD), AX_X,
                                            ALU.add).then_inc(ss_sum_ok, 1)
                    dve.wait_ge(ss_sum_ok, j + 3)
                    nc.vector.tensor_scalar(ss[:], ss[:], QK_EPS, None, ALU.add).then_inc(ss_ok, 1)
                if back:
                    low(ps_h1T, h1T_hi, h1T_lo, h1T_hi_ok, j + 1, h1T_lo_ok)
                if s == -2:
                    dve.wait_ge(mix_hi_ok, 1)
                    nc.vector.tensor_tensor(w_lo[:, :, MIX:], bank01[:, :, 0:D], w_hi[:, :, MIX:].bitcast(F32),
                                            ALU.subtract).then_inc(mix_lo_ok, 1)

            dve.wait_ge(w_hi_ok, 2)
            nc.vector.scalar_tensor_tensor(w_lo[:, :, TOK:QK], w_raw[:, :, 0:D], 1.0 / K,
                                           w_hi[:, :, TOK:QK].bitcast(F32), ALU.mult, ALU.subtract).then_inc(w_lo_ok, 1)
            nc.vector.tensor_tensor(w_lo[:, :, QK:MIX], w_raw[:, :, D:5 * D], w_hi[:, :, QK:MIX].bitcast(F32),
                                    ALU.subtract).then_inc(w_lo_ok, 1)
            dve.wait_ge(pos_mm, 1)
            nc.vector.tensor_copy(pos_rows[:], ps_h).then_inc(pos_ok, 1)
            for c in range(C):
                dve.wait_ge(half_mm, c + 1)
                nc.vector.tensor_copy(half_mix[:, c, :], ps_scores[:, c, :]).then_inc(half_ok, 1)
            low(ps_pT, pT_hi, pT_lo, pT_hi_ok, 1, pT_lo_ok)
            steps(dve, step)

        @block.tensor
        def _(pe):
            def dense(ps, a_hi, a_lo, first, width):
                for c in range(C):
                    for k, (a, w) in enumerate(((a_hi, w_hi), (a_hi, w_lo), (a_lo, w_hi))):
                        mm = nc.tensor.matmul(ps, a[:, c, :], w[:, c, first:first + width],
                                              start=(c == 0 and k == 0), stop=(c == C - 1 and k == 2))
                return mm

            def transpose(ps, src, chunks):
                for c in range(chunks):
                    mm = nc.tensor.transpose(ps[:, c, :], src[:, c * P:(c + 1) * P], ident[:])
                return mm

            pe.wait_ge(const_in, 16 * 6)
            nc.tensor.matmul(ps_h, feat[:], w_pos[:], start=True, stop=True).then_inc(pos_mm, 1)
            pe.wait_ge(ident_ok, 1)
            pe.wait_ge(pooled_ok, 1)
            transpose(ps_pT, pooled, C).then_inc(pT_mm, 1)
            pe.wait_ge(freq_in, 16 * 3)
            for m in range(C):
                for c in range(C):
                    nc.tensor.matmul(ps_scores[:, m, :], w_freq[:, 0, c, m * P:(m + 1) * P], dft_sb[:, c, D:3 * D],
                                     start=(c == 0), stop=False)
                    mm = nc.tensor.matmul(ps_scores[:, m, :], w_freq[:, 1, c, m * P:(m + 1) * P],
                                          dft_sb[:, c, 0:2 * D], start=False, stop=(c == C - 1))
                mm.then_inc(half_mm, 1)

            def step(j, s):
                front, middle, back, mix = phases(s)
                if front:
                    pe.wait_ge(pT_lo_ok, j + 3)
                    if s == -2:
                        pe.wait_ge(w_lo_ok, 2)
                        pe.wait_ge(pos_ok, 1)
                    else:
                        pe.wait_ge(v_ok, j + 2)
                    dense(ps_h, pT_hi, pT_lo, TOK, D).then_inc(h_mm, 1)
                if mix:
                    pe.wait_ge(h1T_lo_ok, j)
                    if back:
                        pe.wait_ge(e_ok, j + 1)
                    if s == 1:
                        pe.wait_ge(mix_lo_ok, 1)
                    dense(ps_mix, h1T_hi, h1T_lo, MIX, D).then_inc(y_mm, 1)

                def weighted(ps, weight):
                    for c in range(C):
                        for r in range(R):
                            for a in range(2):
                                for q in range(S):
                                    rows = slice(q * T, (q + 1) * T)
                                    mm = nc.tensor.matmul(ps[32 * r:32 * r + 32, q, c, :], weight(rows, c * R + r, a),
                                                          e[rows, r, c, a, :], start=(a == 0), stop=(a == 1),
                                                          tile_position=(q * T, 32 * r))
                    return mm

                if back:
                    if not mix:
                        pe.wait_ge(e_ok, j + 1)
                    if mix and not middle:
                        pe.wait_ge(y_ok, j)
                    weighted(ps_den, lambda rows, pair, a: den_sel[rows, a, :]).then_inc(den_mm, 1)
                if middle:
                    pe.wait_ge(qk_n_ok, j + 2)
                    transpose(ps_qkT, qk_n, 2 * C).then_inc(qkT_mm, 1)
                if back:
                    weighted(ps_av, lambda rows, pair, a:
                             v_pad[rows, s % RING, pair, 2 * a:2 * a + 2, :]).then_inc(av_mm, 1)
                if front:
                    pe.wait_ge(xn_ok, j + 3)
                    transpose(ps_hT, xn, C).then_inc(hT_mm, 1)
                if middle:
                    pe.wait_ge(qkT_ok, 3 * (j + 2))
                    if mix:
                        pe.wait_ge(y_ok, j)
                    if back:
                        pe.wait_ge(den_r_ok, j + 1)
                    for c in range(C):
                        for q in range(S):
                            for r in range(R):
                                rows, toks = slice(32 * r, 32 * r + 32), slice(q * T, (q + 1) * T)
                                mm = nc.tensor.matmul(ps_scores[toks, r, c * P:(c + 1) * P], kT[rows, c, toks],
                                                      q_mask[rows, c, :, toks], start=True, stop=True,
                                                      tile_position=(32 * r, q * T))
                    mm.then_inc(scores_mm, 1)
                if back:
                    pe.wait_ge(o_lo_ok, j + 1)
                    dense(ps_attn, o_hi, o_lo, O, D).then_inc(attn_mm, 1)
                if front:
                    if s + 3 < tiles:
                        pe.wait_ge(pooled_ok, j + 4)
                        transpose(ps_pT, pooled, C).then_inc(pT_mm, 1)
                    pe.wait_ge(hT_lo_ok, j + 3)
                    dense(ps_v, hT_hi, hT_lo, V, D).then_inc(v_mm, 1)
                    dense(ps_qk, hT_hi, hT_lo, QK, 2 * D).then_inc(qk_mm, 1)
                if back:
                    pe.wait_ge(xn1_ok, j + 1)
                    transpose(ps_h1T, xn1, C).then_inc(h1T_mm, 1)
                if s == -2:
                    pe.wait_ge(half_ok, C)
                    pe.wait_ge(pT_lo_ok, 2)
                    for n in range(C):
                        for c in range(C):
                            nc.tensor.matmul(bank01[:, n, 0:D], half_mix[:, c, n * P:(n + 1) * P],
                                             dft_sb[:, c, D:2 * D], start=(c == 0), stop=False)
                            mm = nc.tensor.matmul(bank01[:, n, 0:D], half_mix[:, c, D + n * P:D + (n + 1) * P],
                                                  dft_sb[:, c, 2 * D:3 * D], start=False, stop=(c == C - 1))
                    mm.then_inc(mix_mm, 1)
                if s == -1:
                    pe.wait_ge(mix_lo_ok, 1)

            steps(pe, step)


def kernel(x, L0_tok_W, L0_tok_b, L0_attn_Wqkv, L0_attn_Wo, L0_attn_bo,
           L0_ffn_w_freq_real, L0_ffn_w_freq_imag, L0_ffn_bias):
    import concourse.bacc as bacc
    from concourse.bass_utils import run_bass_kernel_spmd

    f32 = np.float32
    n = np.arange(D)
    angle = 2 * np.pi * (np.outer(n, n) % D) / D
    cos, sin = np.cos(angle) / D ** 0.5, np.sin(angle) / D ** 0.5
    dft = np.concatenate([sin, cos, -sin], 1).astype(f32)

    inv_freq = (f32(1.0) / f32(10000.0) ** (np.arange(HD // 2, dtype=f32) / f32(HD // 2))).astype(f32)
    turn = np.tile((np.arange(T, dtype=f32)[:, None] * inv_freq[None, :]).astype(f32), (S, 1))
    c8, s8 = np.cos(turn), np.sin(turn)
    odd = (np.arange(P) // HD % 2)[:, None]
    mask = np.concatenate([1 - odd, odd], 1)
    den = np.zeros((P, 2, 32))
    den[:, 0, 0:HD] = 1
    den[:, 1, HD:] = 1
    consts = np.concatenate([c8, c8, -s8, s8, mask, den.reshape(P, 64)], 1).astype(f32)

    freqs = np.exp(np.linspace(0.0, np.log(1000.0), POS // 2).astype(f32)).astype(f32)
    pos = (np.arange(T, dtype=f32) / f32(T - 1)).astype(f32)
    ang = (pos[:, None] * freqs[None, :]).astype(f32)
    feat = np.concatenate([np.sin(ang), np.cos(ang), np.ones((T, 1))], 1).astype(f32)
    pos_feat = np.ascontiguousarray(np.tile(feat, (S, 1)).T)

    arrays = {
        "x": x, "w_tok": np.ascontiguousarray(np.asarray(L0_tok_W).T), "b_tok": L0_tok_b, "w_qkv": L0_attn_Wqkv,
        "w_o": L0_attn_Wo, "b_o": L0_attn_bo, "w_re": L0_ffn_w_freq_real, "w_im": L0_ffn_w_freq_imag,
        "b_ffn": L0_ffn_bias, "dft": dft, "consts": consts, "pos_feat": pos_feat,
    }
    arrays = {name: np.ascontiguousarray(a) for name, a in arrays.items()}
    nc = bacc.Bacc("TRN2", target_bir_lowering=False, num_devices=1)
    args = [nc.dram_tensor(name, a.shape, mybir.dt.from_np(a.dtype), kind="ExternalInput").ap()
            for name, a in arrays.items()]
    shape = (x.shape[0], T, D)
    out = nc.dram_tensor("out", shape, F32, kind="ExternalOutput").ap()
    audio_tower(nc, *args, out)
    result = run_bass_kernel_spmd(nc, [arrays], core_ids=[0])
    return result.results[0]["out"]
```

```python
from contextlib import ExitStack

import numpy as np

import concourse.bass as bass
from concourse import mybir

F32 = mybir.dt.float32
F32R = mybir.dt.float32r
ALU = mybir.AluOpType
ACT = mybir.ActivationFunctionType
AX_X = mybir.AxisListType.X

P = 128
K = 4
D = 256
C = D // P
T = 64
S = P // T
HD = 16
H = D // HD
G = 2
A = 4
POS = 32
LN_EPS = 1e-5
QK_EPS = 1e-6
RING = 3
MIN_AHEAD, MAX_AHEAD = -1, 6


def audio_tower(nc, x, w_tok, b_tok, w_qkv, w_o, b_o, w_re, w_im, b_ffn, dft, consts, pos_feat, out):
    tiles = x.shape[0] * x.shape[1] * x.shape[2] // (K * D * P)
    x_tiles = x.rearrange("b (t k) d -> (b t) (k d)", k=K).rearrange("(n p) f -> n p f", p=P)
    out_tiles = out.rearrange("b t d -> (b t) d").rearrange("(n p) d -> n p d", p=P)

    with ExitStack() as ctx:
        def sb(name, shape, dt=F32):
            return ctx.enter_context(nc.sbuf_tensor(name, shape, dt))

        def sem(name):
            return ctx.enter_context(nc.semaphore(name))

        def bank(name, shape=(P, 512)):
            return ctx.enter_context(nc.psum_tensor(name, list(shape), F32))

        ps_av = bank("bank_av")[:, 0:D].rearrange("p (c t) -> p c t", c=C)
        bank_den = bank("bank_den")
        ps_den = bank_den[:, 0:D].rearrange("p (c t) -> p c t", c=C)
        bank_h = bank("bank_h")
        ps_h = ps_v = bank_h[:, 0:D]
        ps_hT = bank_h[:, 0:D].rearrange("p (c t) -> p c t", c=C)
        bank_qk = bank("bank_qk")
        ps_qk = bank_qk[:, :]
        ps_scores = bank("bank_scores", (P, G, C, 4 * T))
        ps_qkT = ps_scores[:, 0].rearrange("p a n -> p (a n)").rearrange("p (c t) -> p c t", c=2 * C)
        bank_out = bank("bank_out")
        ps_attn = ps_mix = bank_out[:, 0:D]
        ps_h1T = bank_out[:, 0:D].rearrange("p (c t) -> p c t", c=C)
        ps_half = (ps_scores[:, 0].rearrange('p c n -> p (c n)'), ps_scores[:, 1].rearrange('p c n -> p (c n)'))
        ps_pT = bank("bank_p")[:, 0:D].rearrange("p (c t) -> p c t", c=C)

        ident = sb("ident", [P, P])
        const = sb("const", [P, 2 * HD + A + 64 + 2])
        LN_EPS_COL, QK_EPS_COL = 2 * HD + A + 64, 2 * HD + A + 65
        rope_cos, rope_sin = const[:, 0:HD], const[:, HD:2 * HD]
        head_mask = const[:, 2 * HD:2 * HD + A]
        den_sel = const[:, 2 * HD + A:LN_EPS_COL].rearrange("p (a m) -> p a m", a=2)
        bo_rows = sb("bo_rows", [P, D])
        bf_rows = sb("bf_rows", [P, D])
        w_raw = sb("w_raw", [P, C, D + 3 * D + D])
        w_pos = sb("w_pos", [POS + 1, D])
        feat = sb("feat", [POS + 1, P])
        pos_rows = sb("pos_rows", [P, D])
        dft_sb = sb("dft_sb", [P, C, 3 * D])
        w_freq = sb("w_freq", [P, 2, C, D])
        half_mix = sb("half_mix", [P, C, 2 * D])
        W_ALL = D + 3 * D + D + D
        TOK, QK, V, O, MIX = 0, D, 3 * D, 4 * D, 5 * D
        w_hi = sb("w_hi", [P, C, W_ALL], F32R)
        w_lo = sb("w_lo", [P, C, W_ALL], F32R)

        x_in = sb("x_in", [P, RING, K * D])
        pair_sum = sb("pair_sum", [P, RING, 2 * D])
        pooled = sb("pooled", [P, RING, D])
        pT_hi, pT_lo = sb("pT_hi", [P, RING, C, P], F32R), sb("pT_lo", [P, RING, C, P], F32R)
        h = sb("h", [P, RING, D])
        h_bo = sb("h_bo", [P, RING, D])
        h_bn, h_mv, h_ln, h_rs0, h_nt, h_nu, h_rs = (
            sb(name, [P, RING, width]) for name, width in
            (("h_bn", 6), ("h_mv", 2), ("h_ln", 1), ("h_rs0", 1), ("h_nt", 1), ("h_nu", 1), ("h_rs", 1)))
        xn = sb("xn", [P, RING, D])
        hT_hi, hT_lo = sb("hT_hi", [P, RING, C, P], F32R), sb("hT_lo", [P, RING, C, P], F32R)
        v_pad = sb("v_pad", [P, RING, H // 2, 4, HD])
        sq = sb("sq", [P, 2 * D])
        q_cos, q_sin, q_rot, qk_n = (sb(n, [P, 2 * D]) for n in ("q_cos", "q_sin", "q_rot", "qk_n"))
        ss, ss_ln, ss_rs0, ss_nt, ss_nu, ss_rs = (sb(n, [P, RING, 2 * H]) for n in
                                                  ("ss", "ss_ln", "ss_rs0", "ss_nt", "ss_nu", "ss_rs"))
        kT = sb("kT", [P, C, P])
        q_mask = sb("q_mask", [P, C, A, P])
        e = sb("e", [P, RING, G, C, A, S, T])
        den_ln, den_r0, den_t, den_s = (
            sb(name, [P, RING, D]) for name in ("den_ln", "den_r0", "den_t", "den_s"))
        o_f = sb("o_f", [P, RING, C, P])
        o_hi, o_lo = sb("o_hi", [P, RING, C, P], F32R), sb("o_lo", [P, RING, C, P], F32R)
        h1 = sb("h1", [P, RING, D])
        h1_bf = sb("h1_bf", [P, RING, D])
        g_bn, g_mv, g_ln, g_rs0, g_nt, g_nu, g_rs = (
            sb(name, [P, RING, width]) for name, width in
            (("g_bn", 6), ("g_mv", 2), ("g_ln", 1), ("g_rs0", 1), ("g_nt", 1), ("g_nu", 1), ("g_rs", 1)))
        xn1 = sb("xn1", [P, RING, D])
        h1T_hi, h1T_lo = sb("h1T_hi", [P, RING, C, P], F32R), sb("h1T_lo", [P, RING, C, P], F32R)
        y = sb("y", [P, RING, D])

        const_in = sem("const_in")
        w_in = sem("w_in")
        freq_in = sem("freq_in")
        zeroed = sem("zeroed")
        ident_ok = sem("ident_ok")
        w_hi_ok, w_lo_ok = sem("w_hi_ok"), sem("w_lo_ok")
        mix_hi_ok, mix_lo_ok = sem("mix_hi_ok"), sem("mix_lo_ok")
        pos_mm, pos_ok = sem("pos_mm"), sem("pos_ok")
        half_mm, half_ok, mix_mm = sem("half_mm"), sem("half_ok"), sem("mix_mm")
        x_ok = [sem(f"x_ok{i}") for i in range(RING)]
        out_sent = [sem(f"out_sent{i}") for i in range(RING)]
        pair_ok, pooled_ok = sem("pair_ok"), sem("pooled_ok")
        pT_mm, pT_hi_ok, pT_lo_ok = sem("pT_mm"), sem("pT_hi_ok"), sem("pT_lo_ok")
        h_mm, h_ok, h_bo_ok = sem("h_mm"), sem("h_ok"), sem("h_bo_ok")
        h_bn_ok, h_mv_ok, h_ln_ok, h_rs0_ok, h_nt_ok, h_nu_ok, h_rs_ok = (
            sem(name) for name in ("h_bn_ok", "h_mv_ok", "h_ln_ok", "h_rs0_ok", "h_nt_ok", "h_nu_ok", "h_rs_ok"))
        xn_ok, hT_mm, hT_hi_ok, hT_lo_ok = sem("xn_ok"), sem("hT_mm"), sem("hT_hi_ok"), sem("hT_lo_ok")
        v_mm, v_ok, qk_mm, sq_ok = sem("v_mm"), sem("v_ok"), sem("qk_mm"), sem("sq_ok")
        rope_ok, rot_ok, ss_ok, ss_ln_ok = sem("rope_ok"), sem("rot_ok"), sem("ss_ok"), sem("ss_ln_ok")
        ss_rs0_ok, ss_nt_ok, ss_nu_ok, ss_rs_ok = (
            sem(name) for name in ("ss_rs0_ok", "ss_nt_ok", "ss_nu_ok", "ss_rs_ok"))
        qk_n_ok, qkT_mm, qkT_ok = sem("qk_n_ok"), sem("qkT_mm"), sem("qkT_ok")
        scores_mm, e_ok = sem("scores_mm"), sem("e_ok")
        den_mm, av_mm, den_ln_ok, den_r0_ok, den_t_ok, den_s_ok = (
            sem(name) for name in ("den_mm", "av_mm", "den_ln_ok", "den_r0_ok", "den_t_ok", "den_s_ok"))
        o_f_ok, o_hi_ok, o_lo_ok = sem("o_f_ok"), sem("o_hi_ok"), sem("o_lo_ok")
        attn_mm, h1_ok, h1_bf_ok = sem("attn_mm"), sem("h1_ok"), sem("h1_bf_ok")
        g_bn_ok, g_mv_ok, g_ln_ok, g_rs0_ok, g_nt_ok, g_nu_ok, g_rs_ok = (
            sem(name) for name in ("g_bn_ok", "g_mv_ok", "g_ln_ok", "g_rs0_ok", "g_nt_ok", "g_nu_ok", "g_rs_ok"))
        xn1_ok, h1T_mm, h1T_hi_ok, h1T_lo_ok = sem("xn1_ok"), sem("h1T_mm"), sem("h1T_hi_ok"), sem("h1T_lo_ok")
        y_mm, y_ok = sem("y_mm"), sem("y_ok")

        block = ctx.enter_context(nc.Block())

        START = -MAX_AHEAD
        END = tiles - MIN_AHEAD
        FIRST = RING - MIN_AHEAD
        LAST = FIRST + (tiles - MAX_AHEAD - FIRST) // RING * RING

        def steps(order):
            def step(j, s):
                def at(ahead, job):
                    if 0 <= s + ahead < tiles:
                        job(j + ahead, s + ahead)
                order(at)
            return step

        def run(eng, order):
            step = steps(order)
            for j in range(START, FIRST):
                step(j, j)
            with eng.Fori(FIRST, LAST - RING + 1, RING) as j:
                for u in range(RING):
                    step(j + u, FIRST + u)
            for j in range(LAST, END):
                step(j, j)

        def nth_of_buffer(n, m):
            return (n - m % RING) // RING + 1

        @block.sync
        def _(sp):
            def load(n, m):
                if m >= RING:
                    sp.wait_ge(pooled_ok, n - RING + 1)
                sp.dma_start(x_in[:, m % RING, :], x_tiles[n]).then_inc(x_ok[m % RING], 16)
                if m == 0 and isinstance(n, int):
                    sp.dma_start(w_raw[:, :, 0:D], w_tok[0:D, :].rearrange("(c p) n -> p c n", p=P)).then_inc(w_in, 16)
                    sp.dma_start(w_raw[:, :, D:4 * D], w_qkv.rearrange("(c p) n -> p c n", p=P)).then_inc(w_in, 16)
                    sp.dma_start(w_raw[:, :, 4 * D:5 * D], w_o.rearrange("(c p) n -> p c n", p=P)).then_inc(w_in, 16)

            def store(n, m):
                sp.wait_ge(y_ok, n + 1)
                sp.dma_start(out_tiles[n], y[:, m % RING, :]).then_inc(out_sent[m % RING], 16)

            def order(at):
                at(6, load)
                at(-1, store)

            run(sp, order)
            for n in range(RING):
                sp.wait_ge(out_sent[n], 16 * len(range(n, tiles, RING)))

        @block.gpsimd
        def _(pool):
            nc.gpsimd.memset(ident[:], 0.0).then_inc(zeroed, 1)
            pool.wait_ge(zeroed, 1)
            nc.gpsimd.affine_select(out=ident[:], in_=ident[:], compare_op=ALU.not_equal, fill=1.0, base=0,
                                    pattern=[[-1, P]], channel_multiplier=1).then_inc(ident_ok, 1)
            nc.gpsimd.memset(v_pad[:], 0.0).then_inc(zeroed, 1)
            nc.gpsimd.memset(e[:], 0.0).then_inc(zeroed, 1)

            def pool_frames(n, m):
                pool.wait_ge(x_ok[m % RING], 16 * nth_of_buffer(n, m))
                nc.gpsimd.tensor_tensor(pair_sum[:, m % RING], x_in[:, m % RING, 0:2 * D], x_in[:, m % RING, 2 * D:4 * D],
                                        ALU.add).then_inc(pair_ok, 1)
                if m >= RING:
                    pool.wait_ge(pT_mm, n - RING + 1)
                pool.wait_ge(pair_ok, n + 1)
                nc.gpsimd.tensor_tensor(pooled[:, m % RING], pair_sum[:, m % RING, 0:D], pair_sum[:, m % RING, D:],
                                        ALU.add).then_inc(pooled_ok, 1)

            def residual(n, m):
                if m >= RING:
                    pool.wait_ge(h1_ok, n - RING + 1)
                if m == 0:
                    pool.wait_ge(const_in, 16 * 6)
                pool.wait_ge(h_ok, n + 1)
                nc.gpsimd.tensor_tensor(h_bo[:, m % RING], h[:, m % RING], bo_rows[:], ALU.add).then_inc(h_bo_ok, 1)

            def rotated(n, m):
                if m >= 1:
                    pool.wait_ge(qk_n_ok, n)
                pool.wait_ge(rope_ok, n + 1)
                nc.gpsimd.tensor_tensor(q_rot[:], q_cos[:], q_sin[:], ALU.add).then_inc(rot_ok, 1)

            def normalised(n, m):
                if m >= 1:
                    pool.wait_ge(qkT_mm, n)
                pool.wait_ge(ss_rs_ok, n + 1)
                pool.wait_ge(rot_ok, n + 1)
                nc.gpsimd.tensor_tensor(
                    qk_n[:].rearrange("p (h d) -> p h d", d=HD), q_rot[:].rearrange("p (h d) -> p h d", d=HD),
                    ss_rs[:, m % RING].unsqueeze(2).to_broadcast([P, 2 * H, HD]), ALU.mult).then_inc(qk_n_ok, 1)

            def attn_low(n, m):
                pool.wait_ge(o_hi_ok, n + 1)
                if m >= RING:
                    pool.wait_ge(attn_mm, n - RING + 1)
                nc.gpsimd.tensor_tensor(o_lo[:, m % RING], o_f[:, m % RING], o_hi[:, m % RING].bitcast(F32),
                                        ALU.subtract).then_inc(o_lo_ok, 1)

            def residual1(n, m):
                if m >= RING:
                    pool.wait_ge(y_ok, n - RING + 1)
                pool.wait_ge(h1_ok, n + 1)
                nc.gpsimd.tensor_tensor(h1_bf[:, m % RING], h1[:, m % RING], bf_rows[:], ALU.add).then_inc(h1_bf_ok, 1)

            def order(at):
                at(1, normalised)
                at(-1, attn_low)
                at(0, residual)
                at(-1, residual1)
                at(5, pool_frames)
                at(2, rotated)

            run(pool, order)

        @block.scalar
        def _(act):
            nc.scalar.preload_act_table_set("natural_log_exp_and_others")
            act.dma_start(const[:], consts).then_inc(const_in, 16)
            act.dma_start(feat[:], pos_feat).then_inc(const_in, 16)
            act.dma_start(w_pos[0:POS, :], w_tok[D:D + POS, :]).then_inc(const_in, 16)
            act.dma_start(w_pos[POS:POS + 1, :], b_tok.rearrange("(a n) -> a n", a=1)).then_inc(const_in, 16)
            act.dma_start(bo_rows[:], b_o.rearrange("(a n) -> a n", a=1).to_broadcast([P, D])).then_inc(const_in, 16)
            act.dma_start(bf_rows[:], b_ffn.rearrange("(a n) -> a n", a=1).to_broadcast([P, D])).then_inc(const_in, 16)
            act.dma_start(w_freq[:, 0], w_re.rearrange("(c p) n -> p c n", p=P)).then_inc(freq_in, 16)
            act.dma_start(w_freq[:, 1], w_im.rearrange("(c p) n -> p c n", p=P)).then_inc(freq_in, 16)
            act.dma_start(dft_sb[:], dft.rearrange("(c p) n -> p c n", p=P)).then_inc(freq_in, 16)
            act.wait_ge(w_in, 16 * 3)
            nc.scalar.activation(w_hi[:, :, TOK:QK], w_raw[:, :, 0:D], ACT.Copy, scale=1.0 / K).then_inc(w_hi_ok, 1)
            nc.scalar.activation(w_hi[:, :, QK:O], w_raw[:, :, D:4 * D], ACT.Copy, scale=-0.5).then_inc(w_hi_ok, 1)
            nc.scalar.activation(w_hi[:, :, O:MIX], w_raw[:, :, 4 * D:5 * D], ACT.Copy, scale=-1.0).then_inc(w_hi_ok, 1)

            def high(src, dst, done):
                nc.scalar.activation(dst, src, ACT.Copy).then_inc(done, 1)

            def ln(src, eps_col, dst, src_ok, ln_ok, n):
                act.wait_ge(src_ok, n + 1)
                nc.scalar.activation(dst, src, ACT.Ln, bias=const[:, eps_col:eps_col + 1]).then_inc(ln_ok, 1)

            def exp_of_ln(src, dst, scale, ln_ok, done, n):
                act.wait_ge(ln_ok, n + 1)
                nc.scalar.activation(dst, src, ACT.Exp, scale=scale).then_inc(done, 1)

            def h_guess_ln(n, m):
                if m == 0:
                    act.wait_ge(const_in, 16 * 6)
                ln(h_mv[:, m % RING, 1:2], LN_EPS_COL, h_ln[:, m % RING], h_mv_ok, h_ln_ok, n)

            def h_guess(n, m):
                exp_of_ln(h_ln[:, m % RING], h_rs0[:, m % RING], -0.5, h_ln_ok, h_rs0_ok, n)

            def g_guess_ln(n, m):
                ln(g_mv[:, m % RING, 1:2], LN_EPS_COL, g_ln[:, m % RING], g_mv_ok, g_ln_ok, n)

            def g_guess(n, m):
                exp_of_ln(g_ln[:, m % RING], g_rs0[:, m % RING], -0.5, g_ln_ok, g_rs0_ok, n)

            def ss_guess_ln(n, m):
                ln(ss[:, m % RING], QK_EPS_COL, ss_ln[:, m % RING], ss_ok, ss_ln_ok, n)

            def ss_guess(n, m):
                exp_of_ln(ss_ln[:, m % RING], ss_rs0[:, m % RING], -0.5, ss_ln_ok, ss_rs0_ok, n)

            def den_guess_ln(n, m):
                act.wait_ge(den_mm, n + 1)
                nc.scalar.activation(den_ln[:, m % RING], bank_den[:, 0:D], ACT.Ln).then_inc(den_ln_ok, 1)

            def den_guess(n, m):
                exp_of_ln(den_ln[:, m % RING], den_r0[:, m % RING], -1.0, den_ln_ok, den_r0_ok, n)

            def keys_queries(n, m):
                act.wait_ge(qkT_mm, n + 1)
                nc.scalar.activation(kT[:], ps_qkT[:, C:2 * C, :], ACT.Copy)
                for a in range(A):
                    last = nc.scalar.activation(q_mask[:, :, a, :], ps_qkT[:, 0:C, :], ACT.Copy,
                                                scale=head_mask[:, a:a + 1])
                last.then_inc(qkT_ok, 1)

            def attn_high(n, m):
                act.wait_ge(o_f_ok, n + 1)
                if m >= RING:
                    act.wait_ge(attn_mm, n - RING + 1)
                high(o_f[:, m % RING], o_hi[:, m % RING], o_hi_ok)

            def hT_high(n, m):
                act.wait_ge(hT_mm, n + 1)
                high(ps_hT, hT_hi[:, m % RING], hT_hi_ok)

            def h1T_high(n, m):
                act.wait_ge(h1T_mm, n + 1)
                high(ps_h1T, h1T_hi[:, m % RING], h1T_hi_ok)

            def pT_high(n, m):
                act.wait_ge(pT_mm, n + 1)
                high(ps_pT, pT_hi[:, m % RING], pT_hi_ok)

            def exps(n, m):
                act.wait_ge(scores_mm, n + 1)
                if m == 0:
                    act.wait_ge(zeroed, 3)
                if m >= RING:
                    act.wait_ge(av_mm, n - RING + 1)
                for q in range(S):
                    rows = slice(q * T, (q + 1) * T)
                    nc.scalar.activation(e[rows, m % RING, :, :, :, q, :].rearrange("p g c a t -> p (g c a) t"),
                                         ps_scores[rows].rearrange("p g c (a t) -> p (g c a) t", t=T),
                                         ACT.Exp, scale=HD ** -0.5 / 4).then_inc(e_ok, 1)

            def values(n, m):
                act.wait_ge(v_mm, n + 1)
                if m == 0:
                    act.wait_ge(zeroed, 3)
                if m >= RING:
                    act.wait_ge(av_mm, n - RING + 1)
                nc.scalar.activation(v_pad[:, m % RING, :, 0:4:3, :],
                                     ps_v.rearrange("p (h a d) -> p h a d", a=2, d=HD), ACT.Copy).then_inc(v_ok, 1)

            def squares(n, m):
                act.wait_ge(qk_mm, n + 1)
                if m >= 1:
                    act.wait_ge(ss_ok, n)
                nc.scalar.activation(sq[:], ps_qk, ACT.Square).then_inc(sq_ok, 1)

            def mixing_high(n, m):
                if m == 0:
                    act.wait_ge(mix_mm, 1)
                    nc.scalar.activation(w_hi[:, :, MIX:], bank_out[:, :].rearrange("p (c n) -> p c n", c=C),
                                         ACT.Copy, scale=-0.5).then_inc(mix_hi_ok, 1)

            def order(at):
                at(4, pT_high)
                at(0, den_guess_ln)
                at(1, keys_queries)
                at(2, squares)
                at(0, den_guess)
                at(2, values)
                at(2, ss_guess_ln)
                at(-1, g_guess_ln)
                at(2, ss_guess)
                at(-1, g_guess)
                at(1, exps)
                at(-1, h1T_high)
                at(3, h_guess_ln)
                at(3, h_guess)
                at(3, mixing_high)
                at(0, attn_high)
                at(3, hT_high)

            run(act, order)

        @block.vector
        def _(dve):
            def low(src, hi, dst, hi_ok, n, done):
                dve.wait_ge(hi_ok, n + 1)
                nc.vector.tensor_tensor(dst, src, hi.bitcast(F32), ALU.subtract).then_inc(done, 1)

            def statistics(src, bn, src_ok, bn_ok, n):
                dve.wait_ge(src_ok, n + 1)
                nc.vector.bn_stats(bn, src).then_inc(bn_ok, 1)

            def moments(bn, mv, bn_ok, mv_ok, n):
                dve.wait_ge(pos_ok, 1)
                dve.wait_ge(bn_ok, n + 1)
                nc.vector.bn_aggr(mv, bn).then_inc(mv_ok, 1)

            def newton_a(mv, rs0, nt, rs0_ok, nt_ok, n):
                dve.wait_ge(rs0_ok, n + 1)
                nc.vector.tensor_scalar(nt, mv[:, 1:2], LN_EPS, rs0, ALU.add, ALU.mult).then_inc(nt_ok, 1)

            def newton_b(nt, rs0, nu, nt_ok, nu_ok, n):
                dve.wait_ge(nt_ok, n + 1)
                nc.vector.tensor_scalar(nu, nt, rs0, 3.0, ALU.mult, ALU.subtract).then_inc(nu_ok, 1)

            def newton_c(nu, rs0, rs, nu_ok, rs_ok, n):
                dve.wait_ge(nu_ok, n + 1)
                nc.vector.tensor_tensor(rs, nu, rs0, ALU.mult).then_inc(rs_ok, 1)

            def scaled(src, mv, rs, dst, rs_ok, dst_ok, n):
                dve.wait_ge(rs_ok, n + 1)
                nc.vector.tensor_scalar(dst, src, mv[:, 0:1], rs, ALU.subtract, ALU.mult).then_inc(dst_ok, 1)

            def embed(n, m):
                dve.wait_ge(h_mm, n + 1)
                if m == 0:
                    dve.wait_ge(pos_ok, 1)
                if m >= RING:
                    dve.wait_ge(h_bo_ok, n - RING + 1)
                nc.vector.tensor_tensor(h[:, m % RING], ps_h, pos_rows[:], ALU.add).then_inc(h_ok, 1)

            def h_statistics(n, m):
                statistics(h[:, m % RING], h_bn[:, m % RING], h_ok, h_bn_ok, n)

            def h_moments(n, m):
                moments(h_bn[:, m % RING], h_mv[:, m % RING], h_bn_ok, h_mv_ok, n)

            def h_newton_a(n, m):
                newton_a(h_mv[:, m % RING], h_rs0[:, m % RING], h_nt[:, m % RING], h_rs0_ok, h_nt_ok, n)

            def h_newton_b(n, m):
                newton_b(h_nt[:, m % RING], h_rs0[:, m % RING], h_nu[:, m % RING], h_nt_ok, h_nu_ok, n)

            def h_newton_c(n, m):
                newton_c(h_nu[:, m % RING], h_rs0[:, m % RING], h_rs[:, m % RING], h_nu_ok, h_rs_ok, n)

            def h_scaled(n, m):
                scaled(h[:, m % RING], h_mv[:, m % RING], h_rs[:, m % RING], xn[:, m % RING], h_rs_ok, xn_ok, n)

            def attn_added(n, m):
                dve.wait_ge(attn_mm, n + 1)
                dve.wait_ge(h_bo_ok, n + 1)
                if m >= RING:
                    dve.wait_ge(h1_bf_ok, n - RING + 1)
                nc.vector.tensor_tensor(h1[:, m % RING], ps_attn, h_bo[:, m % RING], ALU.add).then_inc(h1_ok, 1)

            def g_statistics(n, m):
                statistics(h1[:, m % RING], g_bn[:, m % RING], h1_ok, g_bn_ok, n)

            def g_moments(n, m):
                moments(g_bn[:, m % RING], g_mv[:, m % RING], g_bn_ok, g_mv_ok, n)

            def g_newton_a(n, m):
                newton_a(g_mv[:, m % RING], g_rs0[:, m % RING], g_nt[:, m % RING], g_rs0_ok, g_nt_ok, n)

            def g_newton_b(n, m):
                newton_b(g_nt[:, m % RING], g_rs0[:, m % RING], g_nu[:, m % RING], g_nt_ok, g_nu_ok, n)

            def g_newton_c(n, m):
                newton_c(g_nu[:, m % RING], g_rs0[:, m % RING], g_rs[:, m % RING], g_nu_ok, g_rs_ok, n)

            def g_scaled(n, m):
                scaled(h1[:, m % RING], g_mv[:, m % RING], g_rs[:, m % RING], xn1[:, m % RING], g_rs_ok, xn1_ok, n)

            def ss_newton_a(n, m):
                dve.wait_ge(ss_rs0_ok, n + 1)
                nc.vector.tensor_tensor(ss_nt[:, m % RING], ss_rs0[:, m % RING], ss_rs0[:, m % RING],
                                        ALU.mult).then_inc(ss_nt_ok, 1)

            def ss_newton_b(n, m):
                dve.wait_ge(ss_nt_ok, n + 1)
                nc.vector.scalar_tensor_tensor(ss_nu[:, m % RING], ss[:, m % RING], QK_EPS, ss_nt[:, m % RING],
                                               ALU.add, ALU.mult).then_inc(ss_nu_ok, 1)

            def ss_newton_c(n, m):
                dve.wait_ge(ss_nu_ok, n + 1)
                nc.vector.scalar_tensor_tensor(ss_rs[:, m % RING], ss_nu[:, m % RING], 3.0, ss_rs0[:, m % RING],
                                               ALU.subtract, ALU.mult).then_inc(ss_rs_ok, 1)

            def mixed(n, m):
                dve.wait_ge(y_mm, n + 1)
                dve.wait_ge(h1_bf_ok, n + 1)
                if m >= RING:
                    dve.wait_ge(out_sent[m % RING], 16 * nth_of_buffer(n - RING, m - RING))
                nc.vector.tensor_tensor(y[:, m % RING, :], ps_mix, h1_bf[:, m % RING, :], ALU.add).then_inc(y_ok, 1)

            def den_newton_a(n, m):
                dve.wait_ge(den_r0_ok, n + 1)
                nc.vector.tensor_tensor(den_t[:, m % RING], bank_den[:, 0:D], den_r0[:, m % RING], ALU.mult).then_inc(den_t_ok, 1)

            def den_newton_b(n, m):
                dve.wait_ge(den_t_ok, n + 1)
                nc.vector.scalar_tensor_tensor(den_s[:, m % RING], den_t[:, m % RING], 2.0, den_r0[:, m % RING],
                                               ALU.subtract, ALU.mult).then_inc(den_s_ok, 1)

            def attn_normalised(n, m):
                dve.wait_ge(den_s_ok, n + 1)
                dve.wait_ge(av_mm, n + 1)
                if m >= RING:
                    dve.wait_ge(o_lo_ok, n - RING + 1)
                nc.vector.tensor_tensor(o_f[:, m % RING], ps_av, den_s[:, m % RING].rearrange("p (c t) -> p c t", c=C),
                                        ALU.mult).then_inc(o_f_ok, 1)

            def hT_low(n, m):
                low(ps_hT, hT_hi[:, m % RING], hT_lo[:, m % RING], hT_hi_ok, n, hT_lo_ok)

            def h1T_low(n, m):
                low(ps_h1T, h1T_hi[:, m % RING], h1T_lo[:, m % RING], h1T_hi_ok, n, h1T_lo_ok)

            def pT_low(n, m):
                low(ps_pT, pT_hi[:, m % RING], pT_lo[:, m % RING], pT_hi_ok, n, pT_lo_ok)

            def rope_cosine(n, m):
                dve.wait_ge(sq_ok, n + 1)
                if m >= 1:
                    dve.wait_ge(rot_ok, n)
                nc.vector.tensor_tensor(
                    q_cos[:].rearrange("p (h d) -> p h d", d=HD), ps_qk.rearrange("p (h d) -> p h d", d=HD),
                    rope_cos.unsqueeze(1).to_broadcast([P, 2 * H, HD]), ALU.mult)

            def rope_sine(n, m):
                for a in range(2):
                    half = slice(a * HD // 2, (a + 1) * HD // 2)
                    other = slice((1 - a) * HD // 2, (2 - a) * HD // 2)
                    last = nc.vector.tensor_tensor(
                        q_sin[:].rearrange("p (h d) -> p h d", d=HD)[:, :, half],
                        ps_qk.rearrange("p (h d) -> p h d", d=HD)[:, :, other],
                        rope_sin[:, half].unsqueeze(1).to_broadcast([P, 2 * H, HD // 2]), ALU.mult)
                last.then_inc(rope_ok, 1)

            def square_sums(n, m):
                dve.wait_ge(sq_ok, n + 1)
                nc.vector.tensor_reduce(ss[:, m % RING], sq[:].rearrange("p (h d) -> p h d", d=HD), AX_X,
                                        ALU.add).then_inc(ss_ok, 1)

            def mixing_low(n, m):
                if m == 0:
                    dve.wait_ge(mix_hi_ok, 1)
                    nc.vector.scalar_tensor_tensor(w_lo[:, :, MIX:], bank_out[:, :].rearrange("p (c n) -> p c n", c=C),
                                                   -0.5, w_hi[:, :, MIX:].bitcast(F32),
                                                   ALU.mult, ALU.subtract).then_inc(mix_lo_ok, 1)

            for i, (first, end, scale) in enumerate(((TOK, QK, 1.0 / K), (QK, O, -0.5), (O, MIX, -1.0))):
                dve.wait_ge(w_hi_ok, i + 1)
                nc.vector.scalar_tensor_tensor(w_lo[:, :, first:end], w_raw[:, :, first:end], scale,
                                               w_hi[:, :, first:end].bitcast(F32),
                                               ALU.mult, ALU.subtract).then_inc(w_lo_ok, 1)
            dve.wait_ge(pos_mm, 1)
            nc.vector.tensor_copy(pos_rows[:], ps_h).then_inc(pos_ok, 1)

            def half_mixing(n, m):
                if m == 0:
                    for c in range(C):
                        dve.wait_ge(half_mm, c + 1)
                        nc.vector.tensor_copy(half_mix[:, c, :], ps_half[c]).then_inc(half_ok, 1)

            def order(at):
                at(2, hT_low)
                at(-1, attn_added)
                at(4, pT_low)
                at(4, half_mixing)
                at(-1, g_statistics)
                at(-1, g_moments)
                at(2, square_sums)
                at(0, den_newton_a)
                at(2, rope_cosine)
                at(2, ss_newton_a)
                at(-1, g_newton_a)
                at(2, rope_sine)
                at(-1, g_newton_b)
                at(-1, g_newton_c)
                at(3, embed)
                at(-1, g_scaled)
                at(2, ss_newton_b)
                at(3, h_statistics)
                at(0, den_newton_b)
                at(3, h_moments)
                at(2, ss_newton_c)
                at(0, attn_normalised)
                at(-1, h1T_low)
                at(3, h_newton_a)
                at(3, h_newton_b)
                at(3, h_newton_c)
                at(3, h_scaled)
                at(3, mixing_low)
                at(-1, mixed)

            run(dve, order)

        @block.tensor
        def _(pe):
            def dense(ps, a_hi, a_lo, first, width):
                for c in range(C):
                    for k, (a, w) in enumerate(((a_hi, w_hi), (a_hi, w_lo), (a_lo, w_hi))):
                        mm = nc.tensor.matmul(ps, a[:, c, :], w[:, c, first:first + width],
                                              start=(c == 0 and k == 0), stop=(c == C - 1 and k == 2))
                return mm

            def transpose(ps, src, chunks):
                for c in range(chunks):
                    mm = nc.tensor.transpose(ps[:, c, :], src[:, c * P:(c + 1) * P], ident[:])
                return mm

            pe.wait_ge(const_in, 16 * 6)
            nc.tensor.matmul(ps_h, feat[:], w_pos[:], start=True, stop=True).then_inc(pos_mm, 1)
            def half_mixing(n, m):
                if m == 0:
                    pe.wait_ge(freq_in, 16 * 3)
                    for m in range(C):
                        for c in range(C):
                            nc.tensor.matmul(ps_half[m], w_freq[:, 0, c, m * P:(m + 1) * P], dft_sb[:, c, D:3 * D],
                                             start=(c == 0), stop=False)
                            mm = nc.tensor.matmul(ps_half[m], w_freq[:, 1, c, m * P:(m + 1) * P],
                                                  dft_sb[:, c, 0:2 * D], start=False, stop=(c == C - 1))
                        mm.then_inc(half_mm, 1)

            def mixing(n, m):
                if m == 0:
                    pe.wait_ge(half_ok, C)
                    for n in range(C):
                        for c in range(C):
                            nc.tensor.matmul(bank_out[:, n * D:(n + 1) * D], half_mix[:, c, n * P:(n + 1) * P],
                                             dft_sb[:, c, D:2 * D], start=(c == 0), stop=False)
                            mm = nc.tensor.matmul(bank_out[:, n * D:(n + 1) * D],
                                                  half_mix[:, c, D + n * P:D + (n + 1) * P],
                                                  dft_sb[:, c, 2 * D:3 * D], start=False, stop=(c == C - 1))
                    mm.then_inc(mix_mm, 1)

            def pooled_transposed(n, m):
                if m == 0:
                    pe.wait_ge(ident_ok, 1)
                else:
                    pe.wait_ge(pT_lo_ok, n)
                pe.wait_ge(pooled_ok, n + 1)
                transpose(ps_pT, pooled[:, m % RING], C).then_inc(pT_mm, 1)

            def embedding(n, m):
                pe.wait_ge(pT_lo_ok, n + 1)
                if m == 0:
                    pe.wait_ge(w_lo_ok, 1)
                    pe.wait_ge(pos_ok, 1)
                else:
                    pe.wait_ge(v_ok, n)
                dense(ps_h, pT_hi[:, m % RING], pT_lo[:, m % RING], TOK, D).then_inc(h_mm, 1)

            def h_transposed(n, m):
                pe.wait_ge(xn_ok, n + 1)
                transpose(ps_hT, xn[:, m % RING], C).then_inc(hT_mm, 1)

            def v_product(n, m):
                if m == 0:
                    pe.wait_ge(w_lo_ok, 2)
                pe.wait_ge(hT_lo_ok, n + 1)
                dense(ps_v, hT_hi[:, m % RING], hT_lo[:, m % RING], V, D).then_inc(v_mm, 1)

            def qk_product(n, m):
                pe.wait_ge(hT_lo_ok, n + 1)
                if m >= 1:
                    pe.wait_ge(rope_ok, n)
                dense(ps_qk, hT_hi[:, m % RING], hT_lo[:, m % RING], QK, 2 * D).then_inc(qk_mm, 1)

            def qk_transposed(n, m):
                if m == 0:
                    pe.wait_ge(half_ok, C)
                else:
                    pe.wait_ge(e_ok, S * n)
                pe.wait_ge(qk_n_ok, n + 1)
                transpose(ps_qkT, qk_n, 2 * C).then_inc(qkT_mm, 1)

            def scores(n, m):
                if m == 0:
                    pe.wait_ge(half_ok, C)
                count = n + 1 if isinstance(n, int) else pe.snap(n + 1)
                pe.wait_ge(ident_ok, 1)
                pe.wait_ge(qkT_ok, count)
                for c in range(C):
                    for g in range(G):
                        for q in range(S):
                            rows, toks = slice(64 * g, 64 * g + 64), slice(q * T, (q + 1) * T)
                            mm = nc.tensor.matmul(ps_scores[toks, g, c, :], kT[rows, c, toks],
                                                  q_mask[rows, c, :, toks], start=True, stop=True,
                                                  tile_position=(64 * g, q * T))
                mm.then_inc(scores_mm, 1)

            def weighted(ps, m, weight):
                for c in range(C):
                    for odd in range(2):
                        for r in range(P // 32):
                            a = r % 2 * 2 + odd
                            mm = nc.tensor.matmul(ps[32 * r:32 * r + 32, c, :], weight(c * (P // 32) + r, odd),
                                                  e[:, m % RING, r // 2, c, a, :, :], start=(odd == 0),
                                                  stop=(odd == 1), tile_position=(0, 32 * r))
                return mm

            def denominators(n, m):
                pe.wait_ge(e_ok, S * (n + 1))
                if m >= 1:
                    pe.wait_ge(den_t_ok, n)
                weighted(ps_den, m, lambda pair, odd: den_sel[:, odd, :]).then_inc(den_mm, 1)

            def attended(n, m):
                pe.wait_ge(e_ok, S * (n + 1))
                pe.wait_ge(v_ok, n + 1)
                if m >= 1:
                    pe.wait_ge(o_f_ok, n)
                weighted(ps_av, m, lambda pair, odd:
                         v_pad[:, m % RING, pair, 2 * odd:2 * odd + 2, :]).then_inc(av_mm, 1)

            def attn_projection(n, m):
                if m == 0:
                    pe.wait_ge(w_lo_ok, 3)
                    pe.wait_ge(mix_lo_ok, 1)
                else:
                    pe.wait_ge(y_ok, n)
                pe.wait_ge(o_lo_ok, n + 1)
                dense(ps_attn, o_hi[:, m % RING], o_lo[:, m % RING], O, D).then_inc(attn_mm, 1)

            def h1_transposed(n, m):
                pe.wait_ge(xn1_ok, n + 1)
                transpose(ps_h1T, xn1[:, m % RING], C).then_inc(h1T_mm, 1)

            def mix_product(n, m):
                pe.wait_ge(h1T_lo_ok, n + 1)
                dense(ps_mix, h1T_hi[:, m % RING], h1T_lo[:, m % RING], MIX, D).then_inc(y_mm, 1)

            def order(at):
                at(1, qk_transposed)
                at(-1, attn_projection)
                at(2, qk_product)
                at(2, v_product)
                at(1, scores)
                at(3, embedding)
                at(3, mixing)
                at(0, attended)
                at(-1, h1_transposed)
                at(5, pooled_transposed)
                at(5, half_mixing)
                at(1, denominators)
                at(-1, mix_product)
                at(3, h_transposed)

            run(pe, order)


def kernel(x, L0_tok_W, L0_tok_b, L0_attn_Wqkv, L0_attn_Wo, L0_attn_bo,
           L0_ffn_w_freq_real, L0_ffn_w_freq_imag, L0_ffn_bias):
    import concourse.bacc as bacc
    from concourse.bass_utils import run_bass_kernel_spmd

    f32 = np.float32
    n = np.arange(D)
    angle = 2 * np.pi * (np.outer(n, n) % D) / D
    cos, sin = np.cos(angle) / D ** 0.5, np.sin(angle) / D ** 0.5
    dft = np.concatenate([sin, cos, -sin], 1).astype(f32)

    inv_freq = (f32(1.0) / f32(10000.0) ** (np.arange(HD // 2, dtype=f32) / f32(HD // 2))).astype(f32)
    turn = np.tile((np.arange(T, dtype=f32)[:, None] * inv_freq[None, :]).astype(f32), (S, 1))
    c8, s8 = np.cos(turn), np.sin(turn)
    mask = np.arange(P)[:, None] // HD % A == np.arange(A)
    den = np.zeros((P, 2, 32))
    den[:, 0, 0:HD] = 1
    den[:, 1, HD:] = 1
    eps = np.tile(np.array([[LN_EPS, QK_EPS]]), (P, 1))
    consts = np.concatenate([c8, c8, -s8, s8, mask, den.reshape(P, 64), eps], 1).astype(f32)

    freqs = np.exp(np.linspace(0.0, np.log(1000.0), POS // 2).astype(f32)).astype(f32)
    pos = (np.arange(T, dtype=f32) / f32(T - 1)).astype(f32)
    ang = (pos[:, None] * freqs[None, :]).astype(f32)
    feat = np.concatenate([np.sin(ang), np.cos(ang), np.ones((T, 1))], 1).astype(f32)
    pos_feat = np.ascontiguousarray(np.tile(feat, (S, 1)).T)

    arrays = {
        "x": x, "w_tok": np.ascontiguousarray(np.asarray(L0_tok_W).T), "b_tok": L0_tok_b, "w_qkv": L0_attn_Wqkv,
        "w_o": L0_attn_Wo, "b_o": L0_attn_bo, "w_re": L0_ffn_w_freq_real, "w_im": L0_ffn_w_freq_imag,
        "b_ffn": L0_ffn_bias, "dft": dft, "consts": consts, "pos_feat": pos_feat,
    }
    arrays = {name: np.ascontiguousarray(a) for name, a in arrays.items()}
    nc = bacc.Bacc("TRN2", target_bir_lowering=False, num_devices=1)
    args = [nc.dram_tensor(name, a.shape, mybir.dt.from_np(a.dtype), kind="ExternalInput").ap()
            for name, a in arrays.items()]
    shape = (x.shape[0], T, D)
    out = nc.dram_tensor("out", shape, F32, kind="ExternalOutput").ap()
    audio_tower(nc, *args, out)
    result = run_bass_kernel_spmd(nc, [arrays], core_ids=[0])
    return result.results[0]["out"]
```

```python
from contextlib import ExitStack

import numpy as np

import concourse.bass as bass
from concourse import mybir

F32 = mybir.dt.float32
F32R = mybir.dt.float32r
ALU = mybir.AluOpType
ACT = mybir.ActivationFunctionType
AX_X = mybir.AxisListType.X

P = 128
K = 4
D = 256
C = D // P
T = 64
S = P // T
HD = 16
H = D // HD
G = 2
A = 4
POS = 32
LN_EPS = 1e-5
QK_EPS = 1e-6
RING = 3
MIN_AHEAD, MAX_AHEAD = -2, 7


def audio_tower(nc, x, w_tok, b_tok, w_qkv, w_o, b_o, w_re, w_im, b_ffn, dft, consts, pos_feat, out):
    tiles = x.shape[0] * x.shape[1] * x.shape[2] // (K * D * P)
    x_tiles = x.rearrange("b (t k) d -> (b t) (k d)", k=K).rearrange("(n p) f -> n p f", p=P)
    out_tiles = out.rearrange("b t d -> (b t) d").rearrange("(n p) d -> n p d", p=P)

    with ExitStack() as ctx:
        def sb(name, shape, dt=F32):
            return ctx.enter_context(nc.sbuf_tensor(name, shape, dt))

        def sem(name):
            return ctx.enter_context(nc.semaphore(name))

        def bank(name, shape=(P, 512)):
            return ctx.enter_context(nc.psum_tensor(name, list(shape), F32))

        bank_av = bank("bank_av")
        ps_av = bank_av[:, 0:D].rearrange("p (c t) -> p c t", c=C)
        bank_den = bank("bank_den")
        ps_den = bank_den[:, 0:D].rearrange("p (c t) -> p c t", c=C)
        bank_h = bank("bank_h")
        ps_h = ps_v = bank_h[:, 0:D]
        ps_hT = bank_h[:, 0:D].rearrange("p (c t) -> p c t", c=C)
        bank_qk = bank("bank_qk")
        ps_qk = bank_qk[:, :]
        ps_scores = bank("bank_scores", (P, G, C, 4 * T))
        ps_qkT = ps_scores[:, 0].rearrange("p a n -> p (a n)").rearrange("p (c t) -> p c t", c=2 * C)
        bank_out = bank("bank_out")
        ps_attn = ps_mix = bank_out[:, 0:D]
        ps_h1T = bank_out[:, 0:D].rearrange("p (c t) -> p c t", c=C)
        ps_half = (bank_av[:, :], bank_den[:, :])
        ps_pT = bank("bank_p")[:, 0:D].rearrange("p (c t) -> p c t", c=C)

        ident = sb("ident", [P, P])
        SEL, SWAP = 2 * HD + A, 2 * HD + A + S * HD
        LN_EPS_COL, QK_EPS_COL = SWAP + S, SWAP + S + 1
        const = sb("const", [P, QK_EPS_COL + 1])
        rope_cos, rope_sin = const[:, 0:HD], const[:, HD:2 * HD]
        head_mask = const[:, 2 * HD:2 * HD + A]
        den_sel = const[:, SEL:SWAP]
        swap_mask = const[:, SWAP:SWAP + S].bitcast(mybir.dt.uint32)
        bo_rows = sb("bo_rows", [P, D])
        bf_rows = sb("bf_rows", [P, D])
        w_raw = sb("w_raw", [P, C, D + 3 * D + D])
        w_pos = sb("w_pos", [POS + 1, D])
        feat = sb("feat", [POS + 1, P])
        pos_rows = sb("pos_rows", [P, D])
        dft_sb = sb("dft_sb", [P, C, 3 * D])
        w_freq = sb("w_freq", [P, 2, C, D])
        half_mix = sb("half_mix", [P, C, 2 * D])
        W_ALL = D + 3 * D + D + D
        TOK, QK, V, O, MIX = 0, D, 3 * D, 4 * D, 5 * D
        w_hi = sb("w_hi", [P, C, W_ALL], F32R)
        w_lo = sb("w_lo", [P, C, W_ALL], F32R)

        x_in = sb("x_in", [P, RING, K * D])
        pair_sum = sb("pair_sum", [P, RING, 2 * D])
        pooled = sb("pooled", [P, RING, D])
        pT_hi, pT_lo = sb("pT_hi", [P, RING, C, P], F32R), sb("pT_lo", [P, RING, C, P], F32R)
        h = sb("h", [P, RING, D])
        h_bo = sb("h_bo", [P, RING, D])
        h_bn, h_mv, h_ln, h_rs0, h_nt, h_nu, h_rs = (
            sb(name, [P, RING, width]) for name, width in
            (("h_bn", 6), ("h_mv", 2), ("h_ln", 1), ("h_rs0", 1), ("h_nt", 1), ("h_nu", 1), ("h_rs", 1)))
        xn = sb("xn", [P, RING, D])
        hT_hi, hT_lo = sb("hT_hi", [P, RING, C, P], F32R), sb("hT_lo", [P, RING, C, P], F32R)
        v_seq = sb("v_seq", [P, RING, H, S, HD])
        sq = sb("sq", [P, 2 * D])
        qk, q_cos = sb("qk", [P, RING, 2 * D]), sb("q_cos", [P, RING, 2 * D])
        q_sin, q_rot, qk_n = (sb(n, [P, 2 * D]) for n in ("q_sin", "q_rot", "qk_n"))
        ss, ss_ln, ss_rs0, ss_nt, ss_nu, ss_rs = (sb(n, [P, RING, 2 * H]) for n in
                                                  ("ss", "ss_ln", "ss_rs0", "ss_nt", "ss_nu", "ss_rs"))
        kT = sb("kT", [P, C, P])
        q_mask = sb("q_mask", [P, C, A, P])
        e = sb("e", [P, RING, G, C, A * T])
        den_ln, den_r0, den_t, den_s = (
            sb(name, [P, RING, D]) for name in ("den_ln", "den_r0", "den_t", "den_s"))
        o_f, o_swap = sb("o_f", [P, RING, C, S, T]), sb("o_swap", [P, RING, C, S, T])
        o_hi, o_lo = sb("o_hi", [P, RING, C, P], F32R), sb("o_lo", [P, RING, C, P], F32R)
        h1 = sb("h1", [P, RING, D])
        h1_bf = sb("h1_bf", [P, RING, D])
        g_bn, g_mv, g_ln, g_rs0, g_nt, g_nu, g_rs = (
            sb(name, [P, RING, width]) for name, width in
            (("g_bn", 6), ("g_mv", 2), ("g_ln", 1), ("g_rs0", 1), ("g_nt", 1), ("g_nu", 1), ("g_rs", 1)))
        xn1 = sb("xn1", [P, RING, D])
        h1T_hi, h1T_lo = sb("h1T_hi", [P, RING, C, P], F32R), sb("h1T_lo", [P, RING, C, P], F32R)
        y = sb("y", [P, RING, D])

        const_in = sem("const_in")
        pos_in = sem("pos_in")
        tok_in, qkv_in, o_in = sem("tok_in"), sem("qkv_in"), sem("o_in")
        freq_in = sem("freq_in")
        zeroed = sem("zeroed")
        ident_ok = sem("ident_ok")
        tok_hi_ok, qkv_hi_ok, o_hi_w_ok = sem("tok_hi_ok"), sem("qkv_hi_ok"), sem("o_hi_w_ok")
        tok_lo_ok, qkv_lo_ok, o_lo_w_ok = sem("tok_lo_ok"), sem("qkv_lo_ok"), sem("o_lo_w_ok")
        mix_hi_ok, mix_lo_ok = sem("mix_hi_ok"), sem("mix_lo_ok")
        pos_mm, pos_ok = sem("pos_mm"), sem("pos_ok")
        half_mm, half_ok, mix_mm = sem("half_mm"), sem("half_ok"), sem("mix_mm")
        x_ok = [sem(f"x_ok{i}") for i in range(RING)]
        out_sent = [sem(f"out_sent{i}") for i in range(RING)]
        pair_ok, pooled_ok = sem("pair_ok"), sem("pooled_ok")
        pT_mm, pT_hi_ok, pT_lo_ok = sem("pT_mm"), sem("pT_hi_ok"), sem("pT_lo_ok")
        h_mm, h_ok, h_bo_ok = sem("h_mm"), sem("h_ok"), sem("h_bo_ok")
        h_bn_ok, h_mv_ok, h_ln_ok, h_rs0_ok, h_nt_ok, h_nu_ok, h_rs_ok = (
            sem(name) for name in ("h_bn_ok", "h_mv_ok", "h_ln_ok", "h_rs0_ok", "h_nt_ok", "h_nu_ok", "h_rs_ok"))
        xn_ok, hT_mm, hT_hi_ok, hT_lo_ok = sem("xn_ok"), sem("hT_mm"), sem("hT_hi_ok"), sem("hT_lo_ok")
        v_mm, v_ok, qk_mm, sq_ok = sem("v_mm"), sem("v_ok"), sem("qk_mm"), sem("sq_ok")
        qk_ok, cos_ok, sin_ok, rot_ok = sem("qk_ok"), sem("cos_ok"), sem("sin_ok"), sem("rot_ok")
        ss_ok, ss_ln_ok = sem("ss_ok"), sem("ss_ln_ok")
        ss_rs0_ok, ss_nt_ok, ss_nu_ok, ss_rs_ok = (
            sem(name) for name in ("ss_rs0_ok", "ss_nt_ok", "ss_nu_ok", "ss_rs_ok"))
        qk_n_ok, qkT_mm, qkT_ok = sem("qk_n_ok"), sem("qkT_mm"), sem("qkT_ok")
        scores_mm, e_ok = sem("scores_mm"), sem("e_ok")
        den_mm, av_mm, den_ln_ok, den_r0_ok, den_t_ok, den_s_ok = (
            sem(name) for name in ("den_mm", "av_mm", "den_ln_ok", "den_r0_ok", "den_t_ok", "den_s_ok"))
        o_swap_ok, o_placed_ok = sem("o_swap_ok"), sem("o_placed_ok")
        o_f_ok, o_hi_ok, o_lo_ok = sem("o_f_ok"), sem("o_hi_ok"), sem("o_lo_ok")
        attn_mm, h1_ok, h1_bf_ok = sem("attn_mm"), sem("h1_ok"), sem("h1_bf_ok")
        g_bn_ok, g_mv_ok, g_ln_ok, g_rs0_ok, g_nt_ok, g_nu_ok, g_rs_ok = (
            sem(name) for name in ("g_bn_ok", "g_mv_ok", "g_ln_ok", "g_rs0_ok", "g_nt_ok", "g_nu_ok", "g_rs_ok"))
        xn1_ok, h1T_mm, h1T_hi_ok, h1T_lo_ok = sem("xn1_ok"), sem("h1T_mm"), sem("h1T_hi_ok"), sem("h1T_lo_ok")
        y_mm, y_ok = sem("y_mm"), sem("y_ok")

        block = ctx.enter_context(nc.Block())

        START = -MAX_AHEAD
        END = tiles - MIN_AHEAD
        FIRST = RING - MIN_AHEAD
        LAST = FIRST + (tiles - MAX_AHEAD - FIRST) // RING * RING

        def run(eng, order):
            def step(j, s):
                def at(ahead, job):
                    if 0 <= s + ahead < tiles:
                        job(j + ahead, s + ahead)
                order(at)

            for j in range(START, FIRST):
                step(j, j)
            with eng.Fori(FIRST, LAST - RING + 1, RING) as j:
                for u in range(RING):
                    step(j + u, FIRST + u)
            for j in range(LAST, END):
                step(j, j)

        def wait_apart(eng, done, n, met):
            count = n + 1 if isinstance(n, int) else eng.to_reg(n + 1)
            eng.wait_ge(met, 1)
            eng.wait_ge(done, count)

        def nth_of_buffer(n, m):
            return (n - m % RING) // RING + 1

        @block.sync
        def _(sp):
            def load(n, m):
                if m >= RING:
                    sp.wait_ge(pooled_ok, n - RING + 1)
                sp.dma_start(x_in[:, m % RING, :], x_tiles[n]).then_inc(x_ok[m % RING], 16)
                if m == 0:
                    sp.dma_start(w_raw[:, :, 0:D], w_tok[0:D, :].rearrange("(c p) n -> p c n", p=P)).then_inc(tok_in, 16)
                    sp.dma_start(w_raw[:, :, D:4 * D], w_qkv.rearrange("(c p) n -> p c n", p=P)).then_inc(qkv_in, 16)
                if m == 1:
                    sp.dma_start(w_raw[:, :, 4 * D:5 * D], w_o.rearrange("(c p) n -> p c n", p=P)).then_inc(o_in, 16)

            def store(n, m):
                sp.wait_ge(y_ok, n + 1)
                sp.dma_start(out_tiles[n], y[:, m % RING, :]).then_inc(out_sent[m % RING], 16)

            def order(at):
                at(7, load)
                at(-1, store)

            run(sp, order)
            for n in range(RING):
                sp.wait_ge(out_sent[n], 16 * len(range(n, tiles, RING)))

        @block.gpsimd
        def _(pool):
            nc.gpsimd.memset(ident[:], 0.0).then_inc(zeroed, 1)
            pool.wait_ge(zeroed, 1)
            nc.gpsimd.affine_select(out=ident[:], in_=ident[:], compare_op=ALU.not_equal, fill=1.0, base=0,
                                    pattern=[[-1, P]], channel_multiplier=1).then_inc(ident_ok, 1)
            nc.gpsimd.memset(v_seq[:], 0.0).then_inc(zeroed, 1)

            def pool_frames(n, m):
                pool.wait_ge(x_ok[m % RING], 16 * nth_of_buffer(n, m))
                nc.gpsimd.tensor_tensor(pair_sum[:, m % RING], x_in[:, m % RING, 0:2 * D], x_in[:, m % RING, 2 * D:4 * D],
                                        ALU.add).then_inc(pair_ok, 1)
                if m >= RING:
                    pool.wait_ge(pT_mm, n - RING + 1)
                pool.wait_ge(pair_ok, n + 1)
                nc.gpsimd.tensor_tensor(pooled[:, m % RING], pair_sum[:, m % RING, 0:D], pair_sum[:, m % RING, D:],
                                        ALU.add).then_inc(pooled_ok, 1)

            def residual(n, m):
                if m >= RING:
                    pool.wait_ge(h1_ok, n - RING + 1)
                if m == 0:
                    pool.wait_ge(const_in, 16 * 3)
                pool.wait_ge(h_ok, n + 1)
                nc.gpsimd.tensor_tensor(h_bo[:, m % RING], h[:, m % RING], bo_rows[:], ALU.add).then_inc(h_bo_ok, 1)

            def rope_cosine(n, m):
                pool.wait_ge(qk_ok, n + 1)
                nc.gpsimd.tensor_tensor(
                    q_cos[:, m % RING].rearrange("p (h d) -> p h d", d=HD),
                    qk[:, m % RING].rearrange("p (h d) -> p h d", d=HD),
                    rope_cos.unsqueeze(1).to_broadcast([P, 2 * H, HD]), ALU.mult).then_inc(cos_ok, 1)

            def rotated(n, m):
                if m >= 1:
                    pool.wait_ge(qk_n_ok, n)
                pool.wait_ge(sin_ok, n + 1)
                pool.wait_ge(cos_ok, n + 1)
                nc.gpsimd.tensor_tensor(q_rot[:], q_cos[:, m % RING], q_sin[:], ALU.add).then_inc(rot_ok, 1)

            def normalised(n, m):
                if m >= 1:
                    pool.wait_ge(qkT_mm, n)
                pool.wait_ge(ss_rs_ok, n + 1)
                pool.wait_ge(rot_ok, n + 1)
                nc.gpsimd.tensor_tensor(
                    qk_n[:].rearrange("p (h d) -> p h d", d=HD), q_rot[:].rearrange("p (h d) -> p h d", d=HD),
                    ss_rs[:, m % RING].unsqueeze(2).to_broadcast([P, 2 * H, HD]), ALU.mult).then_inc(qk_n_ok, 1)

            def attn_low(n, m):
                pool.wait_ge(o_hi_ok, n + 1)
                if m >= RING:
                    pool.wait_ge(attn_mm, n - RING + 1)
                nc.gpsimd.tensor_tensor(o_lo[:, m % RING], o_f[:, m % RING].rearrange("p c q t -> p c (q t)"), o_hi[:, m % RING].bitcast(F32),
                                        ALU.subtract).then_inc(o_lo_ok, 1)

            def residual1(n, m):
                if m >= RING:
                    pool.wait_ge(y_ok, n - RING + 1)
                pool.wait_ge(h1_ok, n + 1)
                nc.gpsimd.tensor_tensor(h1_bf[:, m % RING], h1[:, m % RING], bf_rows[:], ALU.add).then_inc(h1_bf_ok, 1)

            def order(at):
                at(5, pool_frames)
                at(-2, residual1)
                at(0, residual)
                at(1, rope_cosine)
                at(1, rotated)
                at(1, normalised)
                at(-1, attn_low)

            run(pool, order)

        @block.scalar
        def _(act):
            nc.scalar.preload_act_table_set("natural_log_exp_and_others")
            act.dma_start(feat[:], pos_feat).then_inc(pos_in, 16)
            act.dma_start(w_pos[0:POS, :], w_tok[D:D + POS, :]).then_inc(pos_in, 16)
            act.dma_start(w_pos[POS:POS + 1, :], b_tok.rearrange("(a n) -> a n", a=1)).then_inc(pos_in, 16)
            act.dma_start(const[:], consts).then_inc(const_in, 16)
            act.dma_start(bo_rows[:], b_o.rearrange("(a n) -> a n", a=1).to_broadcast([P, D])).then_inc(const_in, 16)
            act.dma_start(bf_rows[:], b_ffn.rearrange("(a n) -> a n", a=1).to_broadcast([P, D])).then_inc(const_in, 16)
            act.dma_start(w_freq[:, 0], w_re.rearrange("(c p) n -> p c n", p=P)).then_inc(freq_in, 16)
            act.dma_start(w_freq[:, 1], w_im.rearrange("(c p) n -> p c n", p=P)).then_inc(freq_in, 16)
            act.dma_start(dft_sb[:], dft.rearrange("(c p) n -> p c n", p=P)).then_inc(freq_in, 16)
            def weight_high(loaded, first, end, scale, done):
                act.wait_ge(loaded, 16)
                nc.scalar.activation(w_hi[:, :, first:end], w_raw[:, :, first:end], ACT.Copy, scale=scale).then_inc(done, 1)

            def qkv_weight_high(n, m):
                if m == 0:
                    weight_high(qkv_in, QK, O, -0.5, qkv_hi_ok)

            def o_weight_high(n, m):
                if m == 0:
                    weight_high(o_in, O, MIX, -1.0, o_hi_w_ok)

            weight_high(tok_in, TOK, QK, 1.0 / K, tok_hi_ok)

            def high(src, dst, done):
                nc.scalar.activation(dst, src, ACT.Copy).then_inc(done, 1)

            def ln(src, eps_col, dst, src_ok, ln_ok, n):
                act.wait_ge(src_ok, n + 1)
                nc.scalar.activation(dst, src, ACT.Ln, bias=const[:, eps_col:eps_col + 1]).then_inc(ln_ok, 1)

            def exp_of_ln(src, dst, scale, ln_ok, done, n):
                act.wait_ge(ln_ok, n + 1)
                nc.scalar.activation(dst, src, ACT.Exp, scale=scale).then_inc(done, 1)

            def h_guess_ln(n, m):
                if m == 0:
                    act.wait_ge(const_in, 16 * 3)
                ln(h_mv[:, m % RING, 1:2], LN_EPS_COL, h_ln[:, m % RING], h_mv_ok, h_ln_ok, n)

            def h_guess(n, m):
                exp_of_ln(h_ln[:, m % RING], h_rs0[:, m % RING], -0.5, h_ln_ok, h_rs0_ok, n)

            def g_guess_ln(n, m):
                ln(g_mv[:, m % RING, 1:2], LN_EPS_COL, g_ln[:, m % RING], g_mv_ok, g_ln_ok, n)

            def g_guess(n, m):
                exp_of_ln(g_ln[:, m % RING], g_rs0[:, m % RING], -0.5, g_ln_ok, g_rs0_ok, n)

            def ss_guess_ln(n, m):
                ln(ss[:, m % RING], QK_EPS_COL, ss_ln[:, m % RING], ss_ok, ss_ln_ok, n)

            def ss_guess(n, m):
                exp_of_ln(ss_ln[:, m % RING], ss_rs0[:, m % RING], -0.5, ss_ln_ok, ss_rs0_ok, n)

            def den_guess_ln(n, m):
                act.wait_ge(den_mm, n + 1)
                nc.scalar.activation(den_ln[:, m % RING], bank_den[:, 0:D], ACT.Ln).then_inc(den_ln_ok, 1)

            def den_guess(n, m):
                exp_of_ln(den_ln[:, m % RING], den_r0[:, m % RING], -1.0, den_ln_ok, den_r0_ok, n)

            def keys_queries(n, m):
                act.wait_ge(qkT_mm, n + 1)
                nc.scalar.activation(kT[:], ps_qkT[:, C:2 * C, :], ACT.Copy)
                for a in range(A):
                    last = nc.scalar.activation(q_mask[:, :, a, :], ps_qkT[:, 0:C, :], ACT.Copy,
                                                scale=head_mask[:, a:a + 1])
                last.then_inc(qkT_ok, 1)

            def attn_high(n, m):
                act.wait_ge(o_placed_ok, n + 1)
                if m >= RING:
                    act.wait_ge(attn_mm, n - RING + 1)
                high(o_f[:, m % RING].rearrange("p c q t -> p c (q t)"), o_hi[:, m % RING], o_hi_ok)

            def hT_high(n, m):
                act.wait_ge(hT_mm, n + 1)
                high(ps_hT, hT_hi[:, m % RING], hT_hi_ok)

            def h1T_high(n, m):
                act.wait_ge(h1T_mm, n + 1)
                high(ps_h1T, h1T_hi[:, m % RING], h1T_hi_ok)

            def pT_high(n, m):
                act.wait_ge(pT_mm, n + 1)
                high(ps_pT, pT_hi[:, m % RING], pT_hi_ok)

            def exps(n, m):
                act.wait_ge(scores_mm, n + 1)
                if m >= RING:
                    act.wait_ge(av_mm, n - RING + 1)
                nc.scalar.activation(e[:, m % RING], ps_scores[:], ACT.Exp, scale=HD ** -0.5 / 4).then_inc(e_ok, 1)

            def values(n, m):
                act.wait_ge(v_mm, n + 1)
                if m == 0:
                    act.wait_ge(zeroed, 2)
                if m >= RING:
                    act.wait_ge(av_mm, n - RING + 1)
                for q in range(S):
                    rows = slice(q * T, (q + 1) * T)
                    last = nc.scalar.activation(v_seq[rows, m % RING, :, q, :],
                                                ps_v[rows].rearrange("p (h d) -> p h d", d=HD), ACT.Copy)
                last.then_inc(v_ok, 1)

            def squares(n, m):
                act.wait_ge(qk_mm, n + 1)
                if m >= 1:
                    act.wait_ge(ss_ok, n)
                nc.scalar.activation(sq[:], ps_qk, ACT.Square).then_inc(sq_ok, 1)

            def qk_copied(n, m):
                act.wait_ge(qk_mm, n + 1)
                if m >= RING:
                    act.wait_ge(cos_ok, n - RING + 1)
                    act.wait_ge(sin_ok, n - RING + 1)
                nc.scalar.activation(qk[:, m % RING], ps_qk, ACT.Copy).then_inc(qk_ok, 1)

            def mixing_high(n, m):
                if m == 0:
                    act.wait_ge(mix_mm, 1)
                    nc.scalar.activation(w_hi[:, :, MIX:], bank_out[:, :].rearrange("p (c n) -> p c n", c=C),
                                         ACT.Copy, scale=-0.5).then_inc(mix_hi_ok, 1)

            def order(at):
                at(3, o_weight_high)
                at(0, den_guess_ln)
                at(0, den_guess)
                at(3, h_guess_ln)
                at(3, h_guess)
                at(1, keys_queries)
                at(-1, g_guess_ln)
                at(-1, g_guess)
                at(2, squares)
                at(3, hT_high)
                at(2, qk_copied)
                at(2, ss_guess_ln)
                at(5, pT_high)
                at(2, ss_guess)
                at(-1, h1T_high)
                at(3, values)
                at(1, exps)
                at(1, mixing_high)
                at(5, qkv_weight_high)
                at(0, attn_high)

            run(act, order)

        @block.vector
        def _(dve):
            def low(src, hi, dst, hi_ok, n, done):
                dve.wait_ge(hi_ok, n + 1)
                nc.vector.tensor_tensor(dst, src, hi.bitcast(F32), ALU.subtract).then_inc(done, 1)

            def statistics(src, bn, src_ok, bn_ok, n):
                dve.wait_ge(src_ok, n + 1)
                nc.vector.bn_stats(bn, src).then_inc(bn_ok, 1)

            def moments(bn, mv, bn_ok, mv_ok, n):
                wait_apart(dve, bn_ok, n, pos_ok)
                nc.vector.bn_aggr(mv, bn).then_inc(mv_ok, 1)

            def newton_a(mv, rs0, nt, rs0_ok, nt_ok, n):
                dve.wait_ge(rs0_ok, n + 1)
                nc.vector.tensor_scalar(nt, mv[:, 1:2], LN_EPS, rs0, ALU.add, ALU.mult).then_inc(nt_ok, 1)

            def newton_b(nt, rs0, nu, nt_ok, nu_ok, n):
                dve.wait_ge(nt_ok, n + 1)
                nc.vector.tensor_scalar(nu, nt, rs0, 3.0, ALU.mult, ALU.subtract).then_inc(nu_ok, 1)

            def newton_c(nu, rs0, rs, nu_ok, rs_ok, n):
                dve.wait_ge(nu_ok, n + 1)
                nc.vector.tensor_tensor(rs, nu, rs0, ALU.mult).then_inc(rs_ok, 1)

            def scaled(src, mv, rs, dst, rs_ok, dst_ok, n):
                dve.wait_ge(rs_ok, n + 1)
                nc.vector.tensor_scalar(dst, src, mv[:, 0:1], rs, ALU.subtract, ALU.mult).then_inc(dst_ok, 1)

            def embed(n, m):
                dve.wait_ge(h_mm, n + 1)
                if m == 0:
                    dve.wait_ge(pos_ok, 1)
                if m >= RING:
                    dve.wait_ge(h_bo_ok, n - RING + 1)
                nc.vector.tensor_tensor(h[:, m % RING], ps_h, pos_rows[:], ALU.add).then_inc(h_ok, 1)

            def h_statistics(n, m):
                statistics(h[:, m % RING], h_bn[:, m % RING], h_ok, h_bn_ok, n)

            def h_moments(n, m):
                moments(h_bn[:, m % RING], h_mv[:, m % RING], h_bn_ok, h_mv_ok, n)

            def h_newton_a(n, m):
                newton_a(h_mv[:, m % RING], h_rs0[:, m % RING], h_nt[:, m % RING], h_rs0_ok, h_nt_ok, n)

            def h_newton_b(n, m):
                newton_b(h_nt[:, m % RING], h_rs0[:, m % RING], h_nu[:, m % RING], h_nt_ok, h_nu_ok, n)

            def h_newton_c(n, m):
                newton_c(h_nu[:, m % RING], h_rs0[:, m % RING], h_rs[:, m % RING], h_nu_ok, h_rs_ok, n)

            def h_scaled(n, m):
                scaled(h[:, m % RING], h_mv[:, m % RING], h_rs[:, m % RING], xn[:, m % RING], h_rs_ok, xn_ok, n)

            def attn_added(n, m):
                dve.wait_ge(attn_mm, n + 1)
                dve.wait_ge(h_bo_ok, n + 1)
                if m >= RING:
                    dve.wait_ge(h1_bf_ok, n - RING + 1)
                nc.vector.tensor_tensor(h1[:, m % RING], ps_attn, h_bo[:, m % RING], ALU.add).then_inc(h1_ok, 1)

            def g_statistics(n, m):
                statistics(h1[:, m % RING], g_bn[:, m % RING], h1_ok, g_bn_ok, n)

            def g_moments(n, m):
                moments(g_bn[:, m % RING], g_mv[:, m % RING], g_bn_ok, g_mv_ok, n)

            def g_newton_a(n, m):
                newton_a(g_mv[:, m % RING], g_rs0[:, m % RING], g_nt[:, m % RING], g_rs0_ok, g_nt_ok, n)

            def g_newton_b(n, m):
                newton_b(g_nt[:, m % RING], g_rs0[:, m % RING], g_nu[:, m % RING], g_nt_ok, g_nu_ok, n)

            def g_newton_c(n, m):
                newton_c(g_nu[:, m % RING], g_rs0[:, m % RING], g_rs[:, m % RING], g_nu_ok, g_rs_ok, n)

            def g_scaled(n, m):
                scaled(h1[:, m % RING], g_mv[:, m % RING], g_rs[:, m % RING], xn1[:, m % RING], g_rs_ok, xn1_ok, n)

            def ss_newton_a(n, m):
                dve.wait_ge(ss_rs0_ok, n + 1)
                nc.vector.tensor_tensor(ss_nt[:, m % RING], ss_rs0[:, m % RING], ss_rs0[:, m % RING],
                                        ALU.mult).then_inc(ss_nt_ok, 1)

            def ss_newton_b(n, m):
                dve.wait_ge(ss_nt_ok, n + 1)
                nc.vector.scalar_tensor_tensor(ss_nu[:, m % RING], ss[:, m % RING], QK_EPS, ss_nt[:, m % RING],
                                               ALU.add, ALU.mult).then_inc(ss_nu_ok, 1)

            def ss_newton_c(n, m):
                dve.wait_ge(ss_nu_ok, n + 1)
                nc.vector.scalar_tensor_tensor(ss_rs[:, m % RING], ss_nu[:, m % RING], 3.0, ss_rs0[:, m % RING],
                                               ALU.subtract, ALU.mult).then_inc(ss_rs_ok, 1)

            def mixed(n, m):
                dve.wait_ge(y_mm, n + 1)
                dve.wait_ge(h1_bf_ok, n + 1)
                if m >= RING:
                    dve.wait_ge(out_sent[m % RING], 16 * nth_of_buffer(n - RING, m - RING))
                nc.vector.tensor_tensor(y[:, m % RING, :], ps_mix, h1_bf[:, m % RING, :], ALU.add).then_inc(y_ok, 1)

            def den_newton_a(n, m):
                dve.wait_ge(den_r0_ok, n + 1)
                nc.vector.tensor_tensor(den_t[:, m % RING], bank_den[:, 0:D], den_r0[:, m % RING], ALU.mult).then_inc(den_t_ok, 1)

            def den_newton_b(n, m):
                dve.wait_ge(den_t_ok, n + 1)
                nc.vector.scalar_tensor_tensor(den_s[:, m % RING], den_t[:, m % RING], 2.0, den_r0[:, m % RING],
                                               ALU.subtract, ALU.mult).then_inc(den_s_ok, 1)

            def attn_normalised(n, m):
                dve.wait_ge(den_s_ok, n + 1)
                dve.wait_ge(av_mm, n + 1)
                if m >= RING:
                    dve.wait_ge(o_lo_ok, n - RING + 1)
                nc.vector.tensor_tensor(o_f[:, m % RING].rearrange("p c q t -> p (c q t)"), bank_av[:, 0:D],
                                        den_s[:, m % RING], ALU.mult).then_inc(o_f_ok, 1)

            def attn_swapped(n, m):
                wait_apart(dve, o_f_ok, n, pos_ok)
                nc.vector.stream_shuffle(o_swap[:, m % RING], o_f[:, m % RING],
                                         [(p + HD) % (2 * HD) for p in range(2 * HD)]).then_inc(o_swap_ok, 1)

            def attn_placed(n, m):
                wait_apart(dve, o_swap_ok, n, pos_ok)
                for q in range(S):
                    last = nc.vector.copy_predicated(o_f[:, m % RING, :, q, :],
                                                     swap_mask[:, q:q + 1].unsqueeze(2).to_broadcast([P, C, T]),
                                                     o_swap[:, m % RING, :, 1 - q, :])
                last.then_inc(o_placed_ok, 1)

            def hT_low(n, m):
                low(ps_hT, hT_hi[:, m % RING], hT_lo[:, m % RING], hT_hi_ok, n, hT_lo_ok)

            def h1T_low(n, m):
                low(ps_h1T, h1T_hi[:, m % RING], h1T_lo[:, m % RING], h1T_hi_ok, n, h1T_lo_ok)

            def pT_low(n, m):
                low(ps_pT, pT_hi[:, m % RING], pT_lo[:, m % RING], pT_hi_ok, n, pT_lo_ok)

            def rope_sine(n, m):
                dve.wait_ge(qk_ok, n + 1)
                if m >= 1:
                    dve.wait_ge(rot_ok, n)
                for a in range(2):
                    half = slice(a * HD // 2, (a + 1) * HD // 2)
                    other = slice((1 - a) * HD // 2, (2 - a) * HD // 2)
                    last = nc.vector.tensor_tensor(
                        q_sin[:].rearrange("p (h d) -> p h d", d=HD)[:, :, half],
                        qk[:, m % RING].rearrange("p (h d) -> p h d", d=HD)[:, :, other],
                        rope_sin[:, half].unsqueeze(1).to_broadcast([P, 2 * H, HD // 2]), ALU.mult)
                last.then_inc(sin_ok, 1)

            def square_sums(n, m):
                dve.wait_ge(sq_ok, n + 1)
                nc.vector.tensor_reduce(ss[:, m % RING], sq[:].rearrange("p (h d) -> p h d", d=HD), AX_X,
                                        ALU.add).then_inc(ss_ok, 1)

            def mixing_low(n, m):
                if m == 0:
                    dve.wait_ge(mix_hi_ok, 1)
                    nc.vector.scalar_tensor_tensor(w_lo[:, :, MIX:], bank_out[:, :].rearrange("p (c n) -> p c n", c=C),
                                                   -0.5, w_hi[:, :, MIX:].bitcast(F32),
                                                   ALU.mult, ALU.subtract).then_inc(mix_lo_ok, 1)

            def weight_low(high_ok, first, end, scale, done):
                dve.wait_ge(high_ok, 1)
                nc.vector.scalar_tensor_tensor(w_lo[:, :, first:end], w_raw[:, :, first:end], scale,
                                               w_hi[:, :, first:end].bitcast(F32),
                                               ALU.mult, ALU.subtract).then_inc(done, 1)

            def qkv_weight_low(n, m):
                if m == 0:
                    weight_low(qkv_hi_ok, QK, O, -0.5, qkv_lo_ok)

            def o_weight_low(n, m):
                if m == 0:
                    weight_low(o_hi_w_ok, O, MIX, -1.0, o_lo_w_ok)

            def half_copied(c):
                dve.wait_ge(half_mm, c + 1)
                nc.vector.tensor_copy(half_mix[:, c, :], ps_half[c]).then_inc(half_ok, 1)

            def half_mixing_0(n, m):
                if m == 0:
                    half_copied(0)

            def half_mixing_1(n, m):
                if m == 0:
                    half_copied(1)

            weight_low(tok_hi_ok, TOK, QK, 1.0 / K, tok_lo_ok)
            dve.wait_ge(pos_mm, 1)
            nc.vector.tensor_copy(pos_rows[:], ps_h).then_inc(pos_ok, 1)

            def order(at):
                at(3, h_statistics)
                at(3, h_moments)
                at(0, den_newton_a)
                at(-1, attn_added)
                at(3, h_newton_a)
                at(-1, g_statistics)
                at(3, h_newton_b)
                at(3, h_newton_c)
                at(-1, g_moments)
                at(3, h_scaled)
                at(0, den_newton_b)
                at(-1, g_newton_a)
                at(-1, g_newton_b)
                at(3, half_mixing_0)
                at(2, square_sums)
                at(2, half_mixing_1)
                at(-1, g_newton_c)
                at(3, hT_low)
                at(-1, g_scaled)
                at(2, rope_sine)
                at(2, ss_newton_a)
                at(3, o_weight_low)
                at(0, attn_normalised)
                at(-1, h1T_low)
                at(0, mixing_low)
                at(2, ss_newton_b)
                at(0, attn_swapped)
                at(2, ss_newton_c)
                at(5, qkv_weight_low)
                at(0, attn_placed)
                at(5, pT_low)
                at(-1, mixed)
                at(4, embed)

            run(dve, order)

        @block.tensor
        def _(pe):
            def dense(ps, a_hi, a_lo, first, width):
                for c in range(C):
                    for k, (a, w) in enumerate(((a_hi, w_hi), (a_hi, w_lo), (a_lo, w_hi))):
                        mm = nc.tensor.matmul(ps, a[:, c, :], w[:, c, first:first + width],
                                              start=(c == 0 and k == 0), stop=(c == C - 1 and k == 2))
                return mm

            def transpose(ps, src, chunks):
                for c in range(chunks):
                    mm = nc.tensor.transpose(ps[:, c, :], src[:, c * P:(c + 1) * P], ident[:])
                return mm

            pe.wait_ge(pos_in, 16 * 3)
            nc.tensor.matmul(ps_h, feat[:], w_pos[:], start=True, stop=True).then_inc(pos_mm, 1)
            def half_product(k):
                for c in range(C):
                    nc.tensor.matmul(ps_half[k], w_freq[:, 0, c, k * P:(k + 1) * P], dft_sb[:, c, D:3 * D],
                                     start=(c == 0), stop=False)
                    mm = nc.tensor.matmul(ps_half[k], w_freq[:, 1, c, k * P:(k + 1) * P],
                                          dft_sb[:, c, 0:2 * D], start=False, stop=(c == C - 1))
                mm.then_inc(half_mm, 1)

            def half_mixing_0(n, m):
                if m == 0:
                    pe.wait_ge(freq_in, 16 * 3)
                    half_product(0)

            def half_mixing_1(n, m):
                if m == 0:
                    half_product(1)

            def mixing(n, m):
                if m == 0:
                    pe.wait_ge(half_ok, C)
                    for n in range(C):
                        for c in range(C):
                            nc.tensor.matmul(bank_out[:, n * D:(n + 1) * D], half_mix[:, c, n * P:(n + 1) * P],
                                             dft_sb[:, c, D:2 * D], start=(c == 0), stop=False)
                            mm = nc.tensor.matmul(bank_out[:, n * D:(n + 1) * D],
                                                  half_mix[:, c, D + n * P:D + (n + 1) * P],
                                                  dft_sb[:, c, 2 * D:3 * D], start=False, stop=(c == C - 1))
                    mm.then_inc(mix_mm, 1)

            def pooled_transposed(n, m):
                if m == 0:
                    pe.wait_ge(ident_ok, 1)
                else:
                    pe.wait_ge(pT_lo_ok, n)
                pe.wait_ge(pooled_ok, n + 1)
                transpose(ps_pT, pooled[:, m % RING], C).then_inc(pT_mm, 1)

            def embedding(n, m):
                pe.wait_ge(pT_lo_ok, n + 1)
                if m == 0:
                    pe.wait_ge(tok_lo_ok, 1)
                    pe.wait_ge(pos_ok, 1)
                else:
                    pe.wait_ge(v_ok, n)
                dense(ps_h, pT_hi[:, m % RING], pT_lo[:, m % RING], TOK, D).then_inc(h_mm, 1)

            def h_transposed(n, m):
                pe.wait_ge(xn_ok, n + 1)
                transpose(ps_hT, xn[:, m % RING], C).then_inc(hT_mm, 1)

            def v_product(n, m):
                if m == 0:
                    pe.wait_ge(qkv_lo_ok, 1)
                pe.wait_ge(hT_lo_ok, n + 1)
                dense(ps_v, hT_hi[:, m % RING], hT_lo[:, m % RING], V, D).then_inc(v_mm, 1)

            def qk_product(n, m):
                pe.wait_ge(hT_lo_ok, n + 1)
                if m == 0:
                    pe.wait_ge(qkv_lo_ok, 1)
                if m >= 1:
                    pe.wait_ge(qk_ok, n)
                    pe.wait_ge(sq_ok, n)
                dense(ps_qk, hT_hi[:, m % RING], hT_lo[:, m % RING], QK, 2 * D).then_inc(qk_mm, 1)

            def qk_transposed(n, m):
                if m >= 1:
                    pe.wait_ge(e_ok, n)
                pe.wait_ge(qk_n_ok, n + 1)
                transpose(ps_qkT, qk_n, 2 * C).then_inc(qkT_mm, 1)

            def scores(n, m):
                wait_apart(pe, qkT_ok, n, ident_ok)
                for c in range(C):
                    for g in range(G):
                        for q in range(S):
                            rows, toks = slice(64 * g, 64 * g + 64), slice(q * T, (q + 1) * T)
                            mm = nc.tensor.matmul(ps_scores[toks, g, c, :], kT[rows, c, toks],
                                                  q_mask[rows, c, :, toks], start=True, stop=True,
                                                  tile_position=(64 * g, q * T))
                mm.then_inc(scores_mm, 1)

            def denominators(n, m):
                pe.wait_ge(e_ok, n + 1)
                if m == 0:
                    pe.wait_ge(half_ok, C)
                else:
                    pe.wait_ge(den_t_ok, n)
                for r in range(P // 32):
                    first = 2 * (r % 2) * T
                    mm = nc.tensor.matmul(ps_den[32 * r:32 * r + 32], den_sel, e[:, m % RING, r // 2, :, first:first + 2 * T],
                                          start=True, stop=True, tile_position=(0, 32 * r))
                mm.then_inc(den_mm, 1)

            def attended(n, m):
                pe.wait_ge(e_ok, n + 1)
                pe.wait_ge(v_ok, n + 1)
                if m == 0:
                    pe.wait_ge(half_ok, C)
                else:
                    pe.wait_ge(o_f_ok, n)
                for c in range(C):
                    for b in range(2):
                        for r in range(P // 32):
                            first = (2 * (r % 2) + b) * T
                            mm = nc.tensor.matmul(
                                ps_av[32 * r:32 * r + 32, c, b * T:(b + 1) * T],
                                v_seq[:, m % RING, c * H // C + 2 * r + b].rearrange("p q d -> p (q d)"),
                                e[:, m % RING, r // 2, c, first:first + T],
                                start=True, stop=True, tile_position=(0, 32 * r))
                mm.then_inc(av_mm, 1)

            def attn_projection(n, m):
                if m == 0:
                    pe.wait_ge(o_lo_w_ok, 1)
                    pe.wait_ge(mix_lo_ok, 1)
                else:
                    pe.wait_ge(y_ok, n)
                pe.wait_ge(o_lo_ok, n + 1)
                dense(ps_attn, o_hi[:, m % RING], o_lo[:, m % RING], O, D).then_inc(attn_mm, 1)

            def h1_transposed(n, m):
                pe.wait_ge(xn1_ok, n + 1)
                transpose(ps_h1T, xn1[:, m % RING], C).then_inc(h1T_mm, 1)

            def mix_product(n, m):
                pe.wait_ge(h1T_lo_ok, n + 1)
                dense(ps_mix, h1T_hi[:, m % RING], h1T_lo[:, m % RING], MIX, D).then_inc(y_mm, 1)

            def order(at):
                at(1, qk_transposed)
                at(5, pooled_transposed)
                at(-1, attn_projection)
                at(2, qk_product)
                at(2, half_mixing_1)
                at(0, attended)
                at(3, h_transposed)
                at(1, scores)
                at(-1, h1_transposed)
                at(3, v_product)
                at(1, mixing)
                at(-1, mix_product)
                at(4, embedding)
                at(4, half_mixing_0)
                at(1, denominators)

            run(pe, order)


def kernel(x, L0_tok_W, L0_tok_b, L0_attn_Wqkv, L0_attn_Wo, L0_attn_bo,
           L0_ffn_w_freq_real, L0_ffn_w_freq_imag, L0_ffn_bias):
    import concourse.bacc as bacc
    from concourse.bass_utils import run_bass_kernel_spmd

    f32 = np.float32
    n = np.arange(D)
    angle = 2 * np.pi * (np.outer(n, n) % D) / D
    cos, sin = np.cos(angle) / D ** 0.5, np.sin(angle) / D ** 0.5
    dft = np.concatenate([sin, cos, -sin], 1).astype(f32)

    inv_freq = (f32(1.0) / f32(10000.0) ** (np.arange(HD // 2, dtype=f32) / f32(HD // 2))).astype(f32)
    turn = np.tile((np.arange(T, dtype=f32)[:, None] * inv_freq[None, :]).astype(f32), (S, 1))
    c8, s8 = np.cos(turn), np.sin(turn)
    mask = np.arange(P)[:, None] // HD % A == np.arange(A)
    sequence = np.arange(P)[:, None] // T
    sel = np.repeat(sequence == np.arange(S), HD, 1)
    swap = np.arange(P)[:, None] // HD % 2 != np.arange(S)
    eps = np.tile(np.array([[LN_EPS, QK_EPS]]), (P, 1))
    consts = np.concatenate([c8, c8, -s8, s8, mask, sel, swap, eps], 1).astype(f32)

    freqs = np.exp(np.linspace(0.0, np.log(1000.0), POS // 2).astype(f32)).astype(f32)
    pos = (np.arange(T, dtype=f32) / f32(T - 1)).astype(f32)
    ang = (pos[:, None] * freqs[None, :]).astype(f32)
    feat = np.concatenate([np.sin(ang), np.cos(ang), np.ones((T, 1))], 1).astype(f32)
    pos_feat = np.ascontiguousarray(np.tile(feat, (S, 1)).T)

    arrays = {
        "x": x, "w_tok": np.ascontiguousarray(np.asarray(L0_tok_W).T), "b_tok": L0_tok_b, "w_qkv": L0_attn_Wqkv,
        "w_o": L0_attn_Wo, "b_o": L0_attn_bo, "w_re": L0_ffn_w_freq_real, "w_im": L0_ffn_w_freq_imag,
        "b_ffn": L0_ffn_bias, "dft": dft, "consts": consts, "pos_feat": pos_feat,
    }
    arrays = {name: np.ascontiguousarray(a) for name, a in arrays.items()}
    nc = bacc.Bacc("TRN2", target_bir_lowering=False, num_devices=1)
    args = [nc.dram_tensor(name, a.shape, mybir.dt.from_np(a.dtype), kind="ExternalInput").ap()
            for name, a in arrays.items()]
    shape = (x.shape[0], T, D)
    out = nc.dram_tensor("out", shape, F32, kind="ExternalOutput").ap()
    audio_tower(nc, *args, out)
    result = run_bass_kernel_spmd(nc, [arrays], core_ids=[0])
    return result.results[0]["out"]
```
